# Optimizing a Trainium2 kernel written in Bass

```python
import numpy as np
import jax
import jax.numpy as jnp

def _softmax(x, axis=-1):
    return jax.nn.softmax(x, axis=axis)

def _gelu(x):
    return jax.nn.gelu(x, approximate=True)

def _silu(x):
    return jax.nn.silu(x)

def _sigmoid(x):
    return jax.nn.sigmoid(x)

def _layernorm(x, axis=-1, eps=1e-05):
    m = jnp.mean(x, axis=axis, keepdims=True)
    v = jnp.var(x, axis=axis, keepdims=True)
    return (x - m) / jnp.sqrt(v + eps)

def _scatter_add(tgt, idx, src, axis=0):
    return tgt.at[idx].add(src)

def _segment_sum(src, seg, n):
    return jax.ops.segment_sum(src, seg, n)
kernel_name = 'mk_vit_tower_d2_tok_img256_r4_281842'

def setup_inputs(seed: int=0):
    np.random.seed(seed)
    _w = jnp.asarray

    def _rec_inputs():
        import jax
        import jax.numpy as jnp
        _rk = jax.random.key(seed)
        x = -7.10856e-05 + 0.999911 * jax.random.normal(jax.random.fold_in(_rk, 1), (16, 64, 128, 64), jnp.float32)
        return x
    x = _rec_inputs()

    def _L0_tok_setup():
        import jax, jax.numpy as jnp
        import numpy as np
        PATCH_LEN = 16
        STRIDE = 8
        PAD = 8
        key = jax.random.key(seed)
        k1, k2 = jax.random.split(key)
        x = jax.random.normal(k1, (32, 64, 128, 64), dtype=jnp.float32)
        in_feat = 64 * (PATCH_LEN // 2 + 1) * 2
        W = jax.random.normal(k2, (64, in_feat), dtype=jnp.float32) * 0.02
        return {'x': x, 'W': W}
    _L0_tok_all = _L0_tok_setup()
    _L0_tok_in = {k: v for k, v in _L0_tok_all.items() if k in ('W',)}
    del _L0_tok_all

    def _L0_attn_setup():
        import jax, jax.numpy as jnp
        import numpy as np
        DIM = 64
        NUM_HEADS = 8
        WINDOW = 7

        def _rel_bias(bias_table, seq_len):
            w = WINDOW
            coords = jnp.arange(w)
            idx = coords[:, None] - coords[None, :] + (w - 1)
            bias = bias_table[idx]
            if seq_len <= w:
                return bias[:seq_len, :seq_len]
            repeats = (seq_len + w - 1) // w
            bias = jnp.tile(bias, (repeats, repeats))[:seq_len, :seq_len]
            return bias
        key = jax.random.key(seed)
        ks = jax.random.split(key, 6)
        B, N, C = (4, 512, DIM)
        x = jax.random.normal(ks[0], (B, N, C), dtype=jnp.float32)
        qkv_w = jax.random.normal(ks[1], (3 * C, C), dtype=jnp.float32) * 0.02
        qkv_b = jax.random.normal(ks[2], (3 * C,), dtype=jnp.float32) * 0.02
        proj_w = jax.random.normal(ks[3], (C, C), dtype=jnp.float32) * 0.02
        proj_b = jax.random.normal(ks[4], (C,), dtype=jnp.float32) * 0.02
        bias_table = jax.random.normal(ks[5], ((2 * WINDOW - 1) * NUM_HEADS,), dtype=jnp.float32) * 0.02
        return {'x': x, 'qkv_w': qkv_w, 'qkv_b': qkv_b, 'proj_w': proj_w, 'proj_b': proj_b, 'bias_table': bias_table}
    _L0_attn_all = _L0_attn_setup()
    _L0_attn_in = {k: v for k, v in _L0_attn_all.items() if k in ('qkv_w', 'qkv_b', 'proj_w', 'proj_b', 'bias_table')}
    del _L0_attn_all

    def _L0_ffn_setup():
        import jax, jax.numpy as jnp
        import numpy as np
        B, T, IN_DIM = (64, 64, 64)
        HID, OUT_DIM = (128, 64)
        N_LAYERS, N_EXPERTS, N_SHARED = (2, 16, 1)
        key = jax.random.key(seed)
        ks = jax.random.split(key, 10)
        s = 0.02
        x = jax.random.normal(ks[0], (B, T, IN_DIM), dtype=jnp.float32)
        route_id = jax.random.randint(ks[1], (B,), 0, N_EXPERTS)
        Wi = jax.random.normal(ks[2], (HID, IN_DIM), dtype=jnp.float32) * s
        bi = jnp.zeros((HID,), dtype=jnp.float32)
        Wr = jax.random.normal(ks[3], (N_LAYERS, N_EXPERTS, HID, HID), dtype=jnp.float32) * s
        br = jax.random.normal(ks[4], (N_LAYERS, N_EXPERTS, HID), dtype=jnp.float32) * s
        Ws = jax.random.normal(ks[5], (N_LAYERS, N_SHARED, HID, HID), dtype=jnp.float32) * s
        bs = jax.random.normal(ks[6], (N_LAYERS, N_SHARED, HID), dtype=jnp.float32) * s
        Wo = jax.random.normal(ks[7], (OUT_DIM, HID), dtype=jnp.float32) * s
        bo = jnp.zeros((OUT_DIM,), dtype=jnp.float32)
        return {'x': x, 'route_id': route_id, 'Wi': Wi, 'bi': bi, 'Wr': Wr, 'br': br, 'Ws': Ws, 'bs': bs, 'Wo': Wo, 'bo': bo}
    _L0_ffn_all = _L0_ffn_setup()
    _L0_ffn_in = {k: v for k, v in _L0_ffn_all.items() if k in ('route_id', 'Wi', 'bi', 'Wr', 'br', 'Ws', 'bs', 'Wo', 'bo')}
    del _L0_ffn_all

    def _L1_attn_setup():
        import jax, jax.numpy as jnp
        import numpy as np
        NUM_HEADS = 8
        key = jax.random.key(seed)
        k1, k2, k3 = jax.random.split(key, 3)
        B, N, C = (4, 512, 64)
        x = jax.random.normal(k1, (B, N, C), dtype=jnp.float32)
        qkv_w = jax.random.normal(k2, (3 * C, C), dtype=jnp.float32) * C ** (-0.5)
        proj_w = jax.random.normal(k3, (C, C), dtype=jnp.float32) * C ** (-0.5)
        proj_b = jnp.zeros((C,), dtype=jnp.float32)
        return {'x': x, 'qkv_w': qkv_w, 'proj_w': proj_w, 'proj_b': proj_b}
    _L1_attn_all = _L1_attn_setup()
    _L1_attn_in = {k: v for k, v in _L1_attn_all.items() if k in ('qkv_w', 'proj_w', 'proj_b')}
    del _L1_attn_all

    def _L1_ffn_setup():
        import jax, jax.numpy as jnp
        import numpy as np
        B, S, D, E, H, K = (4, 1024, 64, 8, 128, 2)
        key = jax.random.key(seed)
        ks = jax.random.split(key, 6)
        x = jax.random.normal(ks[0], (B, S, D), jnp.float32)
        Wg = jax.random.normal(ks[1], (D, E), jnp.float32) * 0.02
        bg = jnp.zeros((E,), jnp.float32)
        W1 = jax.random.normal(ks[2], (E, D, H), jnp.float32) * 0.02
        b1 = jnp.zeros((E, H), jnp.float32)
        W2 = jax.random.normal(ks[3], (E, H, D), jnp.float32) * 0.02
        b2 = jnp.zeros((E, D), jnp.float32)
        return {'x': x, 'Wg': Wg, 'bg': bg, 'W1': W1, 'b1': b1, 'W2': W2, 'b2': b2}
    _L1_ffn_all = _L1_ffn_setup()
    _L1_ffn_in = {k: v for k, v in _L1_ffn_all.items() if k in ('Wg', 'bg', 'W1', 'b1', 'W2', 'b2')}
    del _L1_ffn_all
    return {'x': x, 'L0_tok_W': _L0_tok_in['W'], 'L0_attn_qkv_w': _L0_attn_in['qkv_w'], 'L0_attn_qkv_b': _L0_attn_in['qkv_b'], 'L0_attn_proj_w': _L0_attn_in['proj_w'], 'L0_attn_proj_b': _L0_attn_in['proj_b'], 'L0_attn_bias_table': _L0_attn_in['bias_table'], 'L0_ffn_route_id': _L0_ffn_in['route_id'], 'L0_ffn_Wi': _L0_ffn_in['Wi'], 'L0_ffn_bi': _L0_ffn_in['bi'], 'L0_ffn_Wr': _L0_ffn_in['Wr'], 'L0_ffn_br': _L0_ffn_in['br'], 'L0_ffn_Ws': _L0_ffn_in['Ws'], 'L0_ffn_bs': _L0_ffn_in['bs'], 'L0_ffn_Wo': _L0_ffn_in['Wo'], 'L0_ffn_bo': _L0_ffn_in['bo'], 'L1_attn_qkv_w': _L1_attn_in['qkv_w'], 'L1_attn_proj_w': _L1_attn_in['proj_w'], 'L1_attn_proj_b': _L1_attn_in['proj_b'], 'L1_ffn_Wg': _L1_ffn_in['Wg'], 'L1_ffn_bg': _L1_ffn_in['bg'], 'L1_ffn_W1': _L1_ffn_in['W1'], 'L1_ffn_b1': _L1_ffn_in['b1'], 'L1_ffn_W2': _L1_ffn_in['W2'], 'L1_ffn_b2': _L1_ffn_in['b2']}

def reference(x, L0_tok_W, L0_attn_qkv_w, L0_attn_qkv_b, L0_attn_proj_w, L0_attn_proj_b, L0_attn_bias_table, L0_ffn_route_id, L0_ffn_Wi, L0_ffn_bi, L0_ffn_Wr, L0_ffn_br, L0_ffn_Ws, L0_ffn_bs, L0_ffn_Wo, L0_ffn_bo, L1_attn_qkv_w, L1_attn_proj_w, L1_attn_proj_b, L1_ffn_Wg, L1_ffn_bg, L1_ffn_W1, L1_ffn_b1, L1_ffn_W2, L1_ffn_b2):
    import jax
    import jax.numpy as jnp

    def _L0_tok_ref(x, W):
        import jax, jax.numpy as jnp
        import numpy as np
        PATCH_LEN = 16
        STRIDE = 8
        PAD = 8
        B, C, T, V = x.shape
        xp = jnp.pad(x, ((0, 0), (0, 0), (0, PAD), (0, 0)), mode='edge')
        Tp = T + PAD
        N = (Tp - PATCH_LEN) // STRIDE + 1
        idx = jnp.arange(N)[:, None] * STRIDE + jnp.arange(PATCH_LEN)[None, :]
        patches = xp[:, :, idx, :]
        patches = jnp.transpose(patches, (0, 4, 2, 3, 1))
        xf = jnp.fft.rfft(patches, axis=-2, norm='ortho')
        F = xf.shape[-2]
        x_real = xf.real.reshape(B, V, N, F * C)
        x_imag = xf.imag.reshape(B, V, N, F * C)
        x_emb = jnp.concatenate([x_real, x_imag], axis=-1)
        x_emb = x_emb @ W.T
        return x_emb.reshape(B, V * N, -1)

    def _L0_attn_ref(x, qkv_w, qkv_b, proj_w, proj_b, bias_table):
        import jax, jax.numpy as jnp
        import numpy as np
        DIM = 64
        NUM_HEADS = 8
        WINDOW = 7

        def _rel_bias(bias_table, seq_len):
            w = WINDOW
            coords = jnp.arange(w)
            idx = coords[:, None] - coords[None, :] + (w - 1)
            bias = bias_table[idx]
            if seq_len <= w:
                return bias[:seq_len, :seq_len]
            repeats = (seq_len + w - 1) // w
            bias = jnp.tile(bias, (repeats, repeats))[:seq_len, :seq_len]
            return bias
        B, N, C = x.shape
        H, hd = (NUM_HEADS, C // NUM_HEADS)
        qkv = x @ qkv_w.T + qkv_b
        qkv = qkv.reshape(B, N, 3, H, hd).transpose(2, 0, 3, 1, 4)
        q, k, v = (qkv[0], qkv[1], qkv[2])
        scale = hd ** (-0.5)
        attn = jnp.einsum('bhnd,bhmd->bhnm', q, k) * scale
        bias = _rel_bias(bias_table, N)
        attn = attn + bias[None, None, :, :]
        attn = jax.nn.softmax(attn, axis=-1)
        out = jnp.einsum('bhnm,bhmd->bhnd', attn, v)
        out = out.transpose(0, 2, 1, 3).reshape(B, N, C)
        return out @ proj_w.T + proj_b

    def _L0_ffn_ref(x, route_id, Wi, bi, Wr, br, Ws, bs, Wo, bo):
        import jax, jax.numpy as jnp
        import numpy as np
        B, T, IN_DIM = (64, 64, 64)
        HID, OUT_DIM = (128, 64)
        N_LAYERS, N_EXPERTS, N_SHARED = (2, 16, 1)
        flat = x.reshape(-1, x.shape[-1])
        n_tok = flat.shape[0]
        route = jnp.repeat(route_id, n_tok // route_id.shape[0])
        h = jax.nn.relu(flat @ Wi.T + bi)
        n_layers, n_experts = (Wr.shape[0], Wr.shape[1])
        for l in range(n_layers):
            shared = (jnp.einsum('nd,shd->snh', h, Ws[l]) + bs[l][:, None, :]).mean(axis=0)
            routed = jnp.zeros_like(h)
            for e in range(n_experts):
                ye = h @ Wr[l, e].T + br[l, e]
                routed = routed + jnp.where((route == e)[:, None], ye, 0.0)
            h = jax.nn.relu(shared + routed + h)
        out = h @ Wo.T + bo
        return out.reshape(*x.shape[:-1], out.shape[-1])

    def _L1_attn_ref(x, qkv_w, proj_w, proj_b):
        import jax, jax.numpy as jnp
        import numpy as np
        NUM_HEADS = 8
        B, N, C = x.shape
        H = NUM_HEADS
        D = C // H
        scale = D ** (-0.5)
        qkv = (x @ qkv_w.T).reshape(B, N, 3, H, D).transpose(2, 0, 3, 1, 4)
        q, k, v = (qkv[0], qkv[1], qkv[2])
        attn = jnp.einsum('bhnd,bhmd->bhnm', q, k) * scale
        attn = jax.nn.softmax(attn, axis=-1)
        out = jnp.einsum('bhnm,bhmd->bhnd', attn, v)
        out = out.transpose(0, 2, 1, 3).reshape(B, N, C)
        return out @ proj_w.T + proj_b

    def _L1_ffn_ref(x, Wg, bg, W1, b1, W2, b2):
        import jax, jax.numpy as jnp
        import numpy as np
        B, S, D, E, H, K = (4, 1024, 64, 8, 128, 2)
        Bv, Sv, Dv = x.shape
        gate_scores = x @ Wg + bg
        _, idx = jax.lax.top_k(gate_scores, K)
        mask = jax.nn.one_hot(idx, E, dtype=x.dtype).sum(axis=-2)
        xf = x.reshape(-1, Dv)
        mf = mask.reshape(-1, E)
        h = jax.nn.gelu(jnp.einsum('td,edh->teh', xf, W1) + b1[None], approximate=False)
        y = jnp.einsum('teh,ehd->ted', h, W2) + b2[None]
        out = jnp.einsum('ted,te->td', y, mf)
        return out.reshape(Bv, Sv, Dv)
    h = _L0_tok_ref(x, L0_tok_W)
    h = h + _L0_attn_ref(_layernorm(h, axis=-1), L0_attn_qkv_w, L0_attn_qkv_b, L0_attn_proj_w, L0_attn_proj_b, L0_attn_bias_table)
    h = h + _L0_ffn_ref(_layernorm(h, axis=-1), L0_ffn_route_id, L0_ffn_Wi, L0_ffn_bi, L0_ffn_Wr, L0_ffn_br, L0_ffn_Ws, L0_ffn_bs, L0_ffn_Wo, L0_ffn_bo)
    h = h + _L1_attn_ref(_layernorm(h, axis=-1), L1_attn_qkv_w, L1_attn_proj_w, L1_attn_proj_b)
    h = h + _L1_ffn_ref(_layernorm(h, axis=-1), L1_ffn_Wg, L1_ffn_bg, L1_ffn_W1, L1_ffn_b1, L1_ffn_W2, L1_ffn_b2)
    return h

_drawn_inputs = setup_inputs


def setup_inputs(seed=0):
    import zlib

    import numpy as np

    out = dict(_drawn_inputs(seed))
    spreads = {'L0_ffn_bi': (0.0, 0.1),
     'L0_ffn_bo': (0.0, 0.1),
     'L1_attn_proj_b': (0.0, 0.1),
     'L1_ffn_bg': (0.0, 0.1),
     'L1_ffn_b1': (0.0, 0.28),
     'L1_ffn_b2': (0.0, 0.1)}
    factors = {'L0_attn_qkv_w': 4.108, 'L0_attn_bias_table': 200.0}
    for name, (base, spread) in spreads.items():
        noise = np.random.default_rng([zlib.crc32(name.encode()), seed]).standard_normal(out[name].shape)
        drawn = base * np.exp(spread * noise) if base else spread * noise
        out[name] = jnp.asarray(drawn.astype(out[name].dtype))
    for name, factor in factors.items():
        out[name] = (out[name] * factor).astype(out[name].dtype)
    return out
```

```python
from contextlib import ExitStack

import concourse.bass as bass
from concourse import mybir

F32 = mybir.dt.float32
BF16 = mybir.dt.bfloat16
I32 = mybir.dt.int32
ALU = mybir.AluOpType
ACT = mybir.ActivationFunctionType
AX = mybir.AxisListType

B, C, T, V_LEN = 16, 64, 128, 64
N_TOK = 1024
P = 128
JT = N_TOK // P
H, HD = 8, 8
HID = 128
E = 8
G = 4
EPS = 1e-5
PARTS = 3
PROD = PARTS * PARTS * HD
WINDOW = 7
K_MAX = 96
K_NAT = 96
K_ALL = K_MAX + PARTS
UNITS = 16
HEAD_GROUPS = [(0, 1, 2), (3, 4, 5), (6, 7)]
UNIT = [(h, half) for hs in HEAD_GROUPS for half in (0, 1) for h in hs]
ACC_OF, ACC_FIRST, ACC_LAST = {}, set(), {}
_u = 0
for _n, (_hs, _half) in enumerate((hs, half) for hs in HEAD_GROUPS for half in (0, 1)):
    ACC_FIRST.add(_u)
    for _ in _hs:
        ACC_OF[_u] = _n
        _u += 1
    ACC_LAST[_u - 1] = _n
N_ACC = 6
ROWS_H = HD + 1
TILES = 8
RING_USES = TILES + 1
DMA_QK = 2 * PARTS * PARTS * 16

SIDE_USES = {
    "TOKA": (1, 1), "TOKB": (1, 0), "TOKC": (1, 0), "TR": (1, 1), "QK": (1, 1), "QV": (1, 0), "COMB": (1, 1),
    "PROJ": (1, 0), "H1": (1, 1), "L0": (1, 1), "L1": (1, 1), "WO": (1, 0), "GATE": (1, 0),
    "MT": (1, 1), "FE8": (0, 1), "OUT": (1, 0), **{f"{n}{e}": (1, 1) for e in range(8) for n in ("FE", "FW")},
}


class Lin:

    def __init__(self, k, c):
        self.k, self.c = k, c

    def __add__(self, n):
        return Lin(self.k + n.k, self.c + n.c) if isinstance(n, Lin) else Lin(self.k, self.c + n)

    __radd__ = __add__

    def __sub__(self, n):
        return self + (-n)

    def __mul__(self, n):
        return Lin(self.k * n, self.c * n)

    __rmul__ = __mul__


def side_schedule(r, f1, f2, f3):
    at = {s / 2: [] for s in range(4 * UNITS)}

    def put(s, name, b, *more):
        at[s].append((name, b, *more))

    put(0, "SCR", r, 1)
    put(0, "VC", r, 1, 0)
    if f2:
        put(0, "LX", r + 2, 0)
    if f1:
        put(1, "COMB", r - 1)
        put(2, "PROJ", r - 1, 1)
        put(2, "LN1", r - 1, "m")
    if f2:
        put(3, "TOKA", r + 2)
    put(2, "RL", r, 1, 0)
    if f1:
        put(3, "LN2", r - 1, "m")
        put(4, "TR", r - 1, "m")
        put(5, "GATE", r - 1)
        put(6, "RANK", r - 1)
        put(7, "MT", r - 1)
        for e in range(9):
            put(8 + e, f"FE{e}", r - 1)
            if e < E:
                put(8.5 + e, f"FW{e}", r - 1)
        put(17, "OUT", r - 1)
    if f2:
        put(4, "LX", r + 2, 1)
        put(5.5, "TOKB", r + 2)
        put(6, "TOKC", r + 2)
    if f3:
        put(12, "WCL", r + 1)
        put(15, "WCA", r + 1)
    if f2:
        put(16, "LN1", r + 2, "0")
        put(17, "LN2", r + 2, "0")
        put(18, "TR", r + 2, "0")
        put(19, "QK", r + 2, 0)
        put(19.5, "QV", r + 2, 0)
        put(21, "SCR", r + 2, 0)
        put(21, "VC", r + 2, 0, UNITS)
        put(23, "RL", r + 2, 0, UNITS)
    put(18, "HO1", r)
    if f3:
        put(17.5, "COMB", r + 1)
        put(18.5, "PROJ", r + 1, 0)
        put(19, "LN1", r + 1, "a")
        put(20, "LN2", r + 1, "a")
        put(20, "BO", r + 1)
        put(21, "TR", r + 1, "a")
        put(22, "H1", r + 1)
        put(23, "L0", r + 1)
        put(24, "L1", r + 1)
        put(25, "WO", r + 1)
        put(26, "LN1", r + 1, "1")
        put(27, "LN2", r + 1, "1")
        put(28, "TR", r + 1, "1")
        put(29, "QK", r + 1, 1)
        put(29.5, "QV", r + 1, 1)
    if f2:
        put(28, "HO0", r + 2)
    return at


def program_phases():
    start = [("LX", 0, 0), ("TOKA", 0), ("LX", 0, 1), ("TOKB", 0), ("TOKC", 0), ("LN1", 0, "0"),
             ("LN2", 0, "0"), ("TR", 0, "0"), ("QK", 0, 0), ("QV", 0, 0), ("SCR", 0, 0), ("VC", 0, 0, 0),
             ("RL", 0, 0, 0), ("HO0", 0)]
    first = {s / 2: [] for s in range(2 * UNITS)}
    first[0] = [("LX", 1, 0)]
    first[3] = [("TOKA", 1), ("LX", 1, 1)]
    first[5] = [("TOKB", 1)]
    first[6] = [("TOKC", 1)]
    first[7] = [("LN1", 1, "0")]
    first[8] = [("LN2", 1, "0")]
    first[9] = [("TR", 1, "0")]
    first[10] = [("QK", 1, 0), ("WCL", 0)]
    first[10.5] = [("QV", 1, 0)]
    first[13] = [("SCR", 1, 0), ("WCA", 0)]
    middle = [("VC", 1, 0, UNITS), ("RL", 1, 0, UNITS), ("COMB", 0), ("PROJ", 0, 0), ("LN1", 0, "a"),
              ("LN2", 0, "a"), ("BO", 0), ("TR", 0, "a"), ("H1", 0), ("L0", 0), ("L1", 0), ("WO", 0),
              ("LN1", 0, "1"), ("LN2", 0, "1"), ("TR", 0, "1"), ("QK", 0, 1), ("QV", 0, 1), ("HO0", 1)]
    last = side_schedule(B - 1, True, False, False)
    tail = [x for s in range(2 * UNITS, 4 * UNITS) for x in last.pop(s / 2) if x[0] != "HO1"]
    v_last = UNITS + 2 * UNITS * (B - 1)
    late = [("SCR", B - 1, 1), ("VC", B - 1, 1, v_last), ("RL", B - 1, 1, v_last)]
    for s in last:
        last[s] = [x for x in last[s] if x[0] not in ("SCR", "VC", "RL")]
    end = tail + [("HO1", B - 1)]
    f1 = side_schedule(B, True, False, False)
    end += [x for s in sorted(f1) for x in f1[s] if x[0] not in ("SCR", "VC", "RL", "HO1")]
    r = Lin(1, 0)
    return [
        ("serial", None, 0, 0, start),
        ("units", (0, 0), 0, 0, first),
        ("serial", None, UNITS, 1, middle),
        ("pair", 0, UNITS, 1, side_schedule(0, False, True, True)),
        ("pair", 1, 3 * UNITS, 1, side_schedule(1, True, True, True)),
        ("loop", r, Lin(2 * UNITS, UNITS), 1, side_schedule(r, True, True, True)),
        ("pair", B - 2, UNITS + 2 * UNITS * (B - 2), 1, side_schedule(B - 2, True, False, True)),
        ("serial", None, v_last, 2, late),
        ("units", (1, B - 1), v_last, 2, last),
        ("serial", None, v_last + UNITS, 2, end),
    ]


LOOP_FROM, LOOP_TO = 2, B - 2


def side_counts(side, before):
    found, now = {}, dict(before)
    steps = side if isinstance(side, dict) else {0: side}
    for s in sorted(steps):
        for n, stage in enumerate(steps[s]):
            found[s, n] = dict(now)
            name = stage[0]
            now[name] = now.get(name, 0) + 1
            uses = SIDE_USES.get(name, (0, 0))
            now["bank0"] = now.get("bank0", 0) + uses[0]
            now["bank1"] = now.get("bank1", 0) + uses[1]
    return found, now


NAMES = ["LX", "TOKA", "TOKB", "TOKC", "LN1", "LN2", "TR", "QK", "QV", "SCR", "VC", "RL", "HO0", "HO1",
         "COMB", "PROJ", "BO", "H1", "L0", "L1", "WO", "GATE", "RANK", "MT", "OUT", "WCL", "WCA",
         "bank0", "bank1"] + [f"{n}{e}" for e in range(9) for n in ("FE", "FW")]


def counted_phases():
    now, out = dict.fromkeys(NAMES, 0), []
    for phase in program_phases():
        side = phase[4]
        if phase[0] == "loop":
            _, after = side_counts(side, dict.fromkeys(NAMES, 0))
            before = {k: Lin(after[k], now[k] - LOOP_FROM * after[k]) for k in NAMES}
            found, _ = side_counts(side, before)
            now = {k: now[k] + (LOOP_TO - LOOP_FROM) * after[k] for k in NAMES}
        else:
            found, now = side_counts(side, now)
        out.append((*phase, found))
    return out


def unit_of(kind, it, s):
    if kind == "units":
        return it[0], it[1], s
    if s < UNITS:
        return 0, it + 1, s
    if s < 2 * UNITS:
        return 1, it, s - UNITS
    return 0, it + 2, s - 2 * UNITS


def tower_kernel(nc, x, w_dft, dft, const, onehot, qk_w, v_w, pw, qk_scale, wi, routed, shared, wo, bo,
                 table, route, wg, w1, b2, w2, out):
    with ExitStack() as ctx:
        def sb(name, shape, dt=F32):
            return ctx.enter_context(nc.sbuf_tensor(name, shape, dt))

        def bank(name):
            return ctx.enter_context(nc.psum_tensor(name, [P, 512], F32))

        def sem(name):
            return ctx.enter_context(nc.semaphore(name))

        QA = [sb(f"q_rows{a}", [K_ALL, H, N_TOK], BF16) for a in (0, 1)]
        KA = [sb(f"k_rows{a}", [K_ALL, H, N_TOK], BF16) for a in (0, 1)]
        VZ = [sb(f"v_padded{a}", [P, JT, H, 32]) for a in (0, 1)]
        prob = sb("prob", [P, 4, 512])
        mx = sb("tile_max", [P, 2, 4, 2])
        neg_max = sb("neg_max", [P, 2, 4])
        mres = sb("max_residue", [P, 2, 4])
        mpart = sb("max_parts", [P, 2, 4, PARTS], BF16)
        mrow = sb("max_rows", [4 * PARTS, 2, P], BF16)
        acc_sb = sb("acc_sb", [P, 3, N_TOK])
        xt = sb("x_rows", [P, 8, 256])
        xe = sb("x_edge", [P, V_LEN])
        AB = sb("patch_halves", [P, N_TOK])
        h0n, h0c, h1n, h1c = (sb(n, [P, JT, 64]) for n in ("h0n", "h0c", "h1n", "h1c"))
        xc, sq = sb("centred", [P, JT, 64]), sb("squares", [P, JT, 64])
        ln_s = sb("ln_s", [P, 5, JT])
        XT = sb("ln_rows", [P, N_TOK])
        QF = sb("qk_f32", [P, N_TOK])
        PT = sb("qk_parts", [P, PARTS, N_TOK], BF16)
        Vn = sb("v_natural", [P, JT, 64])
        rec = sb("reciprocals", [64, 512])
        OT = sb("attn_rows", [P, N_TOK])
        WC = sb("group_weights", [P, G, 2, HID + 1])
        WS = sb("shared_weights", [P, 2, HID + 1])
        HE = sb("hidden", [P, 2, N_TOK])
        mbs = sb("mask_rows", [P, 2, 512])
        ytmp = sb("y_masked", [P, 2, 512])
        yacc = sb("y_sum", [P, 512])
        gs = sb("gate_scores", [P, JT, E])
        rank = sb("gate_rank", [P, JT, E])
        mask = sb("top2_mask", [P, JT, E])
        MTf = sb("mask_t", [P, N_TOK])
        MTb = sb("mask_tb", [P, N_TOK], BF16)
        ot = sb("out_rows", [P, JT, 64])
        n_const = const.shape[1]
        CT = sb("const", [P, n_const])
        ident, comb = CT[:, 0:P], [CT[:, P * (g + 1):P * (g + 2)] for g in range(3)]
        at = 4 * P
        low, upp = CT[:, at:at + 64], CT[:, at + 64:at + 128]
        fold = CT[:, at + 128:at + 192]
        half_pow = CT[:, at + 192:at + 200]
        ident_b = sb("ident_b", [P, P], BF16)
        SEL = sb("expert_rows", [P, E, 64], BF16)
        Wf = sb("w_patch", [P, 4, 2, 64])
        WQK = [sb(f"w_qk{a}", [P, P]) for a in (0, 1)]
        WV = [sb(f"w_v{a}", [P, 64]) for a in (0, 1)]
        WP = [sb(f"w_proj{a}", [P, 64]) for a in (0, 1)]
        scl = sb("qk_scale", [P, 1])
        WI = sb("w_in", [P, HID])
        WO = sb("w_out", [P, 64])
        bob = sb("b_out", [P, 64])
        WG = sb("w_gate", [P, E])
        W1 = sb("w_1", [P, E, HID])
        W2 = sb("w_2", [P, E, 64])
        B2 = sb("b_2", [P, 64])
        dftc = sb("dft", [18, 16])
        T3 = sb("bias_table", [WINDOW, WINDOW])
        routes = sb("routes", [1, B * G], I32)
        scr = [nc.dram_tensor(f"qk_scratch{a}", (PARTS, P, N_TOK), BF16, kind="Internal").ap()
               for a in (0, 1)]

        NAT = [bank("nat0"), bank("nat1")]
        ST = [bank("st0"), bank("st1")]
        ACC = [bank("acc0"), bank("acc1")]
        SIDE = [bank("side0"), bank("side1")]

        s_dma, s_dve, s_pool, s_pe, s_act = (sem(n) for n in
                                             ("set_dma", "set_dve", "set_pool", "set_pe", "set_act"))
        nat_ready, nat_free, negm_ready = sem("nat_ready"), sem("nat_free"), sem("negm_ready")
        mchain, parts_ready, mrow_ready = sem("mchain"), sem("parts_ready"), sem("mrow_ready")
        maxrow_in = [sem("maxrow_in0"), sem("maxrow_in1")]
        st_ready, exp_done, pv_done = sem("st_ready"), sem("exp_done"), sem("pv_done")
        acc_free = sem("acc_free")
        side_full = [sem("side_full0"), sem("side_full1")]
        side_free = [sem("side_free0"), sem("side_free1")]
        x_in, x_used, edge_in, ab_ready = sem("x_in"), sem("x_used"), sem("edge_in"), sem("ab_ready")
        h0n_ready, h1n_ready, ho0, ho1 = sem("h0n_ready"), sem("h1n_ready"), sem("ho0"), sem("ho1")
        ln_d, ln_p, xt_ready, xt_used = sem("ln_d"), sem("ln_p"), sem("xt_ready"), sem("xt_used")
        qk_act, split_p, vn_ready, vc_done = sem("qk_act"), sem("split_p"), sem("vn_ready"), sem("vc_done")
        scr_out = sem("scr_out")
        qk_in = [sem("qk_in0"), sem("qk_in1")]
        tail_d, hres = sem("tail_d"), sem("hres")
        bo_done, hid_ready, wc_in, wc_ready = sem("bo_done"), sem("hid_ready"), sem("wc_in"), sem("wc_ready")
        gate_d, gate_p, mt_ready = sem("gate_d"), sem("gate_p"), sem("mt_ready")
        he_ready, mb_ready, fe_t, y_init, y_add = (sem(n) for n in
                                                  ("he_ready", "mb_ready", "fe_t", "y_init", "y_add"))
        out_ready, out_dma = sem("out_ready"), sem("out_dma")

        sp_passed, pe_passed, pool_passed = sem("sp_passed"), sem("pe_passed"), sem("pool_passed")

        PHASES = counted_phases()
        block = ctx.enter_context(nc.Block())

        def counter(reg):
            def at(n):
                if isinstance(n, Lin):
                    if n.k:
                        assert n.k * LOOP_FROM + n.c > 0 and n.k > 0, (n.k, n.c)
                        return reg[0] * n.k + n.c
                    n = n.c
                return max(n, 0)
            return at

        def run_phases(eng, reg, body):
            for kind, it, v0, grp, side, found in PHASES:
                if kind == "loop":
                    with eng.Fori(LOOP_FROM, LOOP_TO) as r:
                        reg[0] = r
                        body("pair", it, v0, grp, side, found)
                else:
                    body(kind, it, v0, grp, side, found)

        def boundaries(kind, grp, v0, it):
            steps = UNITS if kind == "units" else 2 * UNITS
            starts = kind == "units" or it == 0 and not isinstance(it, Lin)
            ends = kind == "units" or (not isinstance(it, Lin) and it == B - 2)
            return steps, starts, ends

        def vc_index(a, b):
            if a == 1:
                return 2 * b + 3 if isinstance(b, Lin) or b < B - 1 else 2 * b + 2
            return 2 * b if isinstance(b, Lin) or b > 0 else 1

        N_SET_DMA = [0]
        SET_DVE, SET_POOL, SET_PE, SET_ACT = 12, 11, 2, 0

        @block.sync
        def _(eng):
            reg = [None]
            at = counter(reg)

            def alone(_):
                eng.sem_inc(sp_passed, 1)

            n_dma = [0]

            def load(dst, src):
                eng.dma_start(dst, src).then_inc(s_dma, 16)
                n_dma[0] += 16

            load(CT[:, :], const)
            load(dftc[:, :], dft)
            load(acc_sb[0:18, 0:2, :], w_dft[:, 0:32].rearrange("f (a o) c -> f a (o c)", a=2))
            load(HE[0:18, :, :], w_dft[:, 32:64].rearrange("f (a o) c -> f a (o c)", a=2))
            load(prob[0:2 * WINDOW, 0:2, :], onehot.rearrange("r (a c) -> r a c", a=2))
            for c7 in range(WINDOW):
                load(T3[c7:c7 + 1, :], table[WINDOW - 1 - c7:2 * WINDOW - 1 - c7].unsqueeze(0))
            load(scl[:, :], qk_scale)
            load(WI[:, :], wi)
            load(WO[:, :], wo)
            load(bob[:, :], bo.unsqueeze(0).to_broadcast([P, 64]))
            load(WS[:, :, :], shared)
            load(WG[:, :], wg)
            load(W1[:, :, :], w1)
            load(W2[:, :, :], w2)
            load(B2[:, :], b2)
            for a in (0, 1):
                load(WQK[a][:, :], qk_w[a])
                load(WV[a][:, :], v_w[a])
                load(WP[a][:, :], pw[a])
            load(routes[:, :], route.unsqueeze(0))
            N_SET_DMA[0] = n_dma[0]
            eng.wait_ge(s_dve, SET_DVE)
            eng.wait_ge(s_pool, SET_POOL)
            hot = h0c[0:2 * WINDOW, :, :].rearrange("p j c -> p (j c)").bitcast(BF16)
            for h in range(H):
                for s in range(PARTS):
                    row = PROD + WINDOW * s
                    load(QA[0][row:row + WINDOW, h, :], hot[0:WINDOW, :])
                    load(KA[0][row:row + WINDOW, h, :], PT[0:WINDOW, s, :])
            N_SET_DMA.append(n_dma[0])
            eng.wait_ge(s_dma, n_dma[0])

            def max_dma(kind, it, v0, s):
                a, b, u = unit_of(kind, it, s)
                h, half = UNIT[u]
                for q in range(4):
                    c = half * 512 + q * P
                    eng.dma_start(QA[a][K_MAX:K_ALL, h, c:c + P],
                                  mrow[PARTS * q:PARTS * q + PARTS, s % 2, :])\
                        .then_inc(maxrow_in[s % 2], 16)

            def side_stage(stage, n, v0):
                name, b = stage[:2]
                if name == "LX":
                    half = stage[2]
                    alone(eng.wait_ge(x_used, at(2 * b + half)))
                    for hh in range(2):
                        src = x[b if isinstance(b, int) else reg[0] * b.k + b.c].rearrange(
                            "c (m h j) v -> c m h (j v)", h=2, j=4)[:, 8 * half:8 * half + 8, hh]
                        eng.dma_start(xt[64 * hh:64 * hh + 64, :, :], src).then_inc(x_in, 16)
                    if half == 0:
                        item = b if isinstance(b, int) else reg[0] * b.k + b.c
                        for hh in range(2):
                            eng.dma_start(xe[64 * hh:64 * hh + 64, :], x[item][:, T - 1, :])\
                                .then_inc(edge_in, 16)
                elif name == "SCR":
                    a = stage[2]
                    alone(eng.wait_ge(split_p, at(3 * (n["SCR"] + 1))))
                    alone(eng.wait_ge(qk_in[a], at(DMA_QK * b)))
                    eng.dma_start(scr[a].rearrange("i p n -> p i n"), PT[:, :, :]).then_inc(scr_out, 16)
                elif name == "RL":
                    a, at_unit = stage[2:]
                    alone(eng.wait_ge(scr_out, at(16 * (n["RL"] + 1))))
                    alone(eng.wait_ge(st_ready, at(TILES * (v0 + at_unit))))
                    for i in range(PARTS):
                        for j in range(PARTS):
                            row = (PARTS * j + i) * HD
                            eng.dma_start(QA[a][row:row + HD, :, :],
                                          scr[a][i, 0:64, :].rearrange("(h d) n -> d h n", d=HD))\
                                .then_inc(qk_in[a], 16)
                            eng.dma_start(KA[a][row:row + HD, :, :],
                                          scr[a][j, 64:128, :].rearrange("(h d) n -> d h n", d=HD))\
                                .then_inc(qk_in[a], 16)
                elif name == "WCL":
                    alone(eng.wait_ge(hid_ready, at(6 * b)))
                    for g in range(G):
                        idx = b * G + g if isinstance(b, int) else reg[0] * (b.k * G) + (b.c * G + g)
                        e = eng.value_load(routes[0:1, bass.ds(idx, 1)], min_val=0, max_val=15)
                        eng.dma_start(WC[:, g, :, :], routed[bass.ds(e, 1)].squeeze(0)).then_inc(wc_in, 16)
                elif name == "OUT":
                    item = b if isinstance(b, int) else reg[0] * b.k + b.c
                    alone(eng.wait_ge(out_ready, at(b + 1)))
                    eng.dma_start(out[item].rearrange("(p j) d -> p j d", j=JT), ot[:, :, :])\
                        .then_inc(out_dma, 16)

            def body(kind, it, v0, grp, side, found):
                if kind == "serial":
                    for n, stage in enumerate(side):
                        side_stage(stage, found[0, n], v0 if stage[0] not in ("RL", "VC") else 0)
                    return
                steps, starts, ends = boundaries(kind, grp, v0, it)
                if starts:
                    alone(eng.wait_ge(mrow_ready, at(v0 + 2 + 2 * grp + 1)))
                    max_dma(kind, it, v0, 0)
                for s in range(steps):
                    if not (ends and s + 1 >= steps):
                        alone(eng.wait_ge(mrow_ready, at(v0 + (s + 1) + 2 + 2 * grp + 1)))
                        max_dma(kind, it, v0, s + 1)
                    for part in (s, s + 0.5):
                        for n, stage in enumerate(side[part]):
                            side_stage(stage, found[part, n], v0)

            run_phases(eng, reg, body)
            alone(eng.wait_ge(out_dma, at(16 * B)))

        @block.tensor
        def _(eng):
            reg = [None]
            at = counter(reg)
            eng.wait_ge(s_dma, N_SET_DMA[0])
            for part, w in enumerate((acc_sb, HE)):
                wv = w[0:18, 0:2, :].rearrange("f a (o c) -> f a o c", c=64)
                for o in range(32):
                    for c in (0, 64):
                        mm = eng.matmul(SIDE[part][c:c + 64, o * 16:o * 16 + 16], wv[:, o // 16, o % 16, :],
                                        dftc[:, :], start=(o == 0), stop=True, skip_group_check=True)
                mm.then_inc(s_pe, 1)
            for a in range(2):
                mm = eng.matmul(NAT[a][0:WINDOW, :], T3[:, :], prob[0:WINDOW, a, :], start=True, stop=True)
                mm.then_inc(s_pe, 1)
            eng.wait_ge(s_dve, SET_DVE)
            eng.wait_ge(s_pool, SET_POOL)
            eng.wait_ge(s_dma, N_SET_DMA[1])

            def side_bank(n, k, use=0, passed=None):
                eng.wait_ge(side_free[k], at(n[f"bank{k}"] + use))
                if passed is not None:
                    eng.sem_inc(passed, 1)
                return SIDE[k]

            def tok_block(n, dst, cols, rhs):
                for j in range(4):
                    mm = eng.matmul(dst[:, 0:cols], Wf[:, j, :, :].rearrange("p a o -> p (a o)"), rhs(j),
                                    start=(j == 0), stop=(j == 3))
                return mm

            def side_stage(stage, n):
                name, b = stage[:2]
                if name in ("TOKA", "TOKB"):
                    half = name == "TOKB"
                    eng.wait_ge(x_in, at(32 * (2 * b + half + 1)))
                    mm = None
                    if not half:
                        eng.wait_ge(edge_in, at(32 * (b + 1)))
                        tok_block(n, side_bank(n, 1), 64, lambda j: xe[:, :]).then_inc(side_full[1], 1)
                    bk = side_bank(n, 0)
                    xv = xt[:, :, :].rearrange("p m (j v) -> p m j v", j=4)
                    for j in range(4):
                        mm = eng.matmul(bk[:, :], Wf[:, j, :, :].rearrange("p a o -> p (a o)"),
                                        xv[:, :, j, :], start=(j == 0), stop=(j == 3))
                    mm.then_inc(side_full[0], 1)
                elif name == "TOKC":
                    eng.wait_ge(ab_ready, at(3 * (b + 1)))
                    bk = side_bank(n, 0)
                    for j in range(JT):
                        mm = eng.matmul(bk[:, j * 64:j * 64 + 64], AB[:, j * P:j * P + P], fold,
                                        start=(j == 0), stop=True, skip_group_check=True)
                    mm.then_inc(side_full[0], 1)
                elif name == "TR":
                    eng.wait_ge(ln_p, at(6 * (n["TR"] + 1)))
                    eng.sem_inc(pe_passed, 1)
                    for k in range(2):
                        bk = side_bank(n, k, 0, pe_passed)
                        for j in range(4):
                            mm = eng.transpose(bk[0:64, j * P:j * P + P], xc[:, 4 * k + j, :], ident)
                        mm.then_inc(side_full[k], 1)
                elif name == "QK":
                    a = stage[2]
                    eng.wait_ge(xt_ready, at(2 * n["TR"]))
                    for k in range(2):
                        bk = side_bank(n, k)
                        eng.matmul(bk[:, :], WQK[a][:, :], XT[:, k * 512:k * 512 + 512],
                                   start=True, stop=True).then_inc(side_full[k], 1)
                elif name == "QV":
                    a = stage[2]
                    bk = side_bank(n, 0)
                    for j in range(JT):
                        mm = eng.matmul(bk[:, j * 64:j * 64 + 64], XT[:, j * P:j * P + P], WV[a][:, :],
                                        start=(j == 0), stop=True, skip_group_check=True)
                    mm.then_inc(side_full[0], 1)
                elif name == "COMB":
                    eng.wait_ge(acc_free, at(N_ACC * (n["COMB"] + 1)))
                    for k in range(2):
                        bk = side_bank(n, k)
                        for g in range(3):
                            mm = eng.matmul(bk[:, :], comb[g], acc_sb[:, g, k * 512:k * 512 + 512],
                                            start=(g == 0), stop=(g == 2))
                        mm.then_inc(side_full[k], 1)
                elif name == "PROJ":
                    eng.wait_ge(tail_d, at(4 * (n["PROJ"] + 1)))
                    bk = side_bank(n, 0)
                    for j in range(JT):
                        mm = eng.matmul(bk[:, j * 64:j * 64 + 64], OT[:, j * P:j * P + P], WP[stage[2]][:, :],
                                        start=(j == 0), stop=True, skip_group_check=True)
                    mm.then_inc(side_full[0], 1)
                elif name == "H1":
                    eng.wait_ge(xt_ready, at(2 * n["TR"]))
                    xg = XT[:, :].rearrange("p (j q) -> p j q", j=JT)
                    for k in range(2):
                        bk = side_bank(n, k)
                        for g in (2 * k, 2 * k + 1):
                            c = (g % 2) * 256
                            mm = eng.matmul(bk[:, c:c + 256], WI[:, :], xg[:, :, 32 * g:32 * g + 32],
                                            start=(g % 2 == 0), stop=True, skip_group_check=True)
                        mm.then_inc(side_full[k], 1)
                elif name in ("L0", "L1"):
                    ll = int(name[1])
                    eng.wait_ge(wc_ready, at(b + 1))
                    for k in range(2):
                        eng.wait_ge(hid_ready, at(6 * b + 2 * ll + 1 + k))
                        bk = side_bank(n, k)
                        for g in (2 * k, 2 * k + 1):
                            c = (g % 2) * 256
                            mm = eng.matmul(bk[:, c:c + 256], WC[:, g, ll, 0:HID], HE[:, ll, g * 256:g * 256 + 256],
                                            start=(g % 2 == 0), stop=True, skip_group_check=True)
                        mm.then_inc(side_full[k], 1)
                elif name == "WO":
                    eng.wait_ge(hid_ready, at(6 * (b + 1)))
                    bk = side_bank(n, 0)
                    for j in range(JT):
                        mm = eng.matmul(bk[:, j * 64:j * 64 + 64], HE[:, 0, j * P:j * P + P], WO[:, :],
                                        start=(j == 0), stop=True, skip_group_check=True)
                    mm.then_inc(side_full[0], 1)
                elif name == "GATE":
                    eng.wait_ge(xt_ready, at(2 * n["TR"]))
                    bk = side_bank(n, 0)
                    for j in range(JT):
                        mm = eng.matmul(bk[:, j * E:j * E + E], XT[:, j * P:j * P + P], WG[:, :],
                                        start=(j == 0), stop=True, skip_group_check=True)
                    mm.then_inc(side_full[0], 1)
                elif name == "MT":
                    eng.wait_ge(gate_d, at(5 * (b + 1)))
                    eng.sem_inc(pe_passed, 1)
                    for k in range(2):
                        bk = side_bank(n, k, 0, pe_passed)
                        for j in range(4):
                            mm = eng.transpose(bk[0:E, j * P:j * P + P], mask[:, 4 * k + j, :], ident)
                        mm.then_inc(side_full[k], 1)
                elif name.startswith("FE"):
                    e = int(name[2:])
                    if e == 0:
                        eng.wait_ge(mt_ready, at(4 * (b + 1)))
                    if e < E:
                        bk = side_bank(n, 0)
                        for k in range(2):
                            mm = eng.matmul(bk[64 * k:64 * k + 64, :], SEL[:, e, :],
                                            MTb[:, k * 512:k * 512 + 512], start=True, stop=True)
                        mm.then_inc(side_full[0], 1)
                    bk = side_bank(n, 1)
                    if e > 0:
                        eng.wait_ge(he_ready, at(16 * b + 2 * e))
                    for k in range(2):
                        w, m = (B2[:, :], MTf[:, k * 512:k * 512 + 512]) if e == 0 else \
                            (W2[:, e - 1, :], HE[:, (e - 1) % 2, k * 512:k * 512 + 512])
                        mm = eng.matmul(bk[64 * k:64 * k + 64, :], w, m, start=True, stop=True)
                    mm.then_inc(side_full[1], 1)
                elif name.startswith("FW"):
                    e = int(name[2:])
                    for k in range(2):
                        bk = side_bank(n, k)
                        eng.matmul(bk[:, :], W1[:, e, :], XT[:, k * 512:k * 512 + 512],
                                   start=True, stop=True).then_inc(side_full[k], 1)
                elif name == "OUT":
                    eng.wait_ge(y_add, at(8 * (b + 1)))
                    eng.sem_inc(pe_passed, 1)
                    bk = side_bank(n, 0, 0, pe_passed)
                    for j in range(4):
                        mm = eng.transpose(bk[:, j * P:j * P + P], yacc[:, j * P:j * P + P], ident)
                    mm.then_inc(side_full[0], 1)

            def parts_turn(idx, s, v):
                eng.wait_ge(nat_free, at(idx - 1))
                eng.matmul(NAT[s[0]][0:4 * PARTS, 0:P], mpart[:, s[1], :, :].rearrange("p q i -> p (q i)"),
                           ident_b[:, :], start=True, stop=True).then_inc(nat_ready, 1)

            def turn_in(v0, grp, s, real, last=False):
                idx = RING_USES * v0 + (RING_USES * s + 2 * grp if not last else RING_USES * (s - 1) + 2 * grp + 1)
                par = (RING_USES * s + 2 * grp if not last else RING_USES * (s - 1) + 1) % 2
                if real:
                    eng.wait_ge(parts_ready, at(v0 + s - 1))
                parts_turn(idx, (par, s % 2), None)

            def nat(kind, it, v0, grp, s, k):
                a, b, u = unit_of(kind, it, s)
                h, half = UNIT[u]
                if u == 0 and k == 0:
                    eng.wait_ge(qk_in[a], at(DMA_QK * (b + 1)))
                use = RING_USES * s + 2 * grp + 1 + k
                eng.wait_ge(nat_free, at(RING_USES * v0 + use - 1))
                c, kh = half * 512 + (k // 2) * P, k % 2
                eng.matmul(NAT[use % 2][:, :], QA[a][0:K_NAT, h, c:c + P],
                           KA[a][0:K_NAT, h, kh * 512:kh * 512 + 512], start=True, stop=True)\
                    .then_inc(nat_ready, 1)

            def scores(kind, it, v0, s, t):
                a, b, u = unit_of(kind, it, s)
                h, half = UNIT[u]
                if t == 0:
                    if isinstance(v0, Lin):
                        units = Lin(v0.k // 2, v0.c // 2) + s // 2 + 1
                    else:
                        units = v0 // 2 + s // 2 + 1
                    eng.wait_ge(maxrow_in[s % 2], at(64 * units))
                eng.wait_ge(exp_done, at(TILES * (v0 + s) + t - 1))
                eng.matmul(ST[t % 2][:, :], KA[a][0:K_ALL, h, t * P:t * P + P],
                           QA[a][0:K_ALL, h, half * 512:half * 512 + 512], start=True, stop=True)\
                    .then_inc(st_ready, 1)

            def pv(a, b, u, v, si, t):
                h, half = UNIT[u]
                acc = ACC_OF[u]
                if u == 0 and t == 0:
                    eng.wait_ge(vc_done, at(vc_index(a, b)))
                eng.wait_ge(exp_done, at(TILES * v + t + 1))
                if u in ACC_FIRST and t == 0:
                    eng.wait_ge(acc_free, at(N_ACC * si + acc - 1))
                c = 32 * (t % 4)
                mm = eng.matmul(ACC[acc % 2][c:c + 32, :], VZ[a][:, t, h, :], prob[:, t % 4, :],
                                start=(u in ACC_FIRST and t < 4), stop=(u in ACC_LAST and t >= 4),
                                skip_group_check=True)
                mm.then_inc(pv_done, 1)

            def body(kind, it, v0, grp, side, found):
                if kind == "serial":
                    for n, stage in enumerate(side):
                        side_stage(stage, found[0, n])
                    return
                steps, starts, ends = boundaries(kind, grp, v0, it)
                si0 = Lin(v0.k // UNITS, v0.c // UNITS) if isinstance(v0, Lin) else v0 // UNITS
                if starts:
                    for s in range(3):
                        turn_in(v0, grp, s, s == 2)
                        for k in range(TILES):
                            nat(kind, it, v0, grp, s, k)

                def pv_at(s, t):
                    if s < 0:
                        if not starts:
                            pv(1, it - 1, UNITS - 1, v0 - 1, si0 - 1, t)
                        return
                    a, b, u = unit_of(kind, it, s)
                    pv(a, b, u, v0 + s, si0 + s // UNITS, t)

                for s in range(steps):
                    ahead = s + 3
                    has_nat = not (ends and ahead >= steps)
                    if not (ends and s + 1 >= steps):
                        turn_in(v0, grp, ahead, True, last=(ends and s + 2 == steps))
                    for t in range(TILES):
                        if has_nat:
                            nat(kind, it, v0, grp, ahead, t)
                        scores(kind, it, v0, s, t)
                        pv_at(*((s, t - 2) if t >= 2 else (s - 1, t + TILES - 2)))
                        if t in (2, 5):
                            part = s + (t == 5) / 2
                            for n, stage in enumerate(side[part]):
                                side_stage(stage, found[part, n])
                if ends:
                    pv_at(steps - 1, TILES - 2)
                    pv_at(steps - 1, TILES - 1)

            run_phases(eng, reg, body)

        @block.scalar
        def _(eng):
            reg = [None]
            at = counter(reg)
            eng.wait_ge(s_dve, SET_DVE)
            eng.wait_ge(s_pool, SET_POOL)
            eng.wait_ge(s_dma, N_SET_DMA[1])

            def full(n, k, use=0):
                eng.wait_ge(side_full[k], at(n[f"bank{k}"] + use + 1))
                return SIDE[k]

            by_patch = AB[:, :].rearrange("p (j v n) -> p j v n", j=JT, n=2)

            def half_patches(bk, half):
                v = bk[:, :].rearrange("p (m v) -> p m v", m=8)
                eng.activation(by_patch[0:64, :, :, half], v[0:64], ACT.Copy)
                if half == 1:
                    eng.activation(by_patch[64:P, JT - 1, :, 0], v[64:P, 0, :], ACT.Copy)
                return eng.activation(by_patch[64:P, 0:JT - 1, :, half], v[64:P, 1:8, :], ACT.Copy)

            def side_stage(stage, n):
                name, b = stage[:2]
                if name == "TOKA":
                    eng.wait_ge(h0n_ready, at(b))
                    bk = full(n, 1)
                    eng.activation(by_patch[64:P, JT - 1, :, 1], bk[64:P, 0:64], ACT.Copy)\
                        .then_inc(side_free[1], 1)
                    eng.wait_ge(side_free[1], at(n["bank1"] + 1))
                    half_patches(full(n, 0), 0).then_inc(side_free[0], 1)
                    eng.wait_ge(side_free[0], at(n["bank0"] + 1))
                    eng.sem_inc(ab_ready, 2)
                    eng.sem_inc(x_used, 1)
                elif name == "TOKB":
                    half_patches(full(n, 0), 1).then_inc(side_free[0], 1)
                    eng.wait_ge(side_free[0], at(n["bank0"] + 1))
                    eng.sem_inc(ab_ready, 1)
                    eng.sem_inc(x_used, 1)
                elif name == "TR":
                    eng.wait_ge(xt_used, at(n["TR"]))
                    for k in range(2):
                        bk = full(n, k)
                        eng.activation(XT[0:64, k * 512:k * 512 + 512], bk[0:64, :], ACT.Copy)\
                            .then_inc(side_free[k], 1)
                    eng.wait_ge(side_free[0], at(n["bank0"] + 1))
                    eng.wait_ge(side_free[1], at(n["bank1"] + 1))
                    eng.sem_inc(xt_ready, 2)
                elif name == "QK":
                    eng.wait_ge(split_p, at(3 * n["QK"]))
                    eng.wait_ge(scr_out, at(16 * n["QK"]))
                    for k in range(2):
                        bk = full(n, k)
                        c = k * 512
                        eng.activation(QF[:, c:c + 512], bk[:, :], ACT.Copy, scale=scl[:, 0:1])\
                            .then_inc(qk_act, 1)
                        eng.activation(PT[:, 0, c:c + 512], bk[:, :], ACT.Copy, scale=scl[:, 0:1])\
                            .then_inc(side_free[k], 1)
                    eng.wait_ge(side_free[0], at(n["bank0"] + 1))
                    eng.wait_ge(side_free[1], at(n["bank1"] + 1))
                    eng.sem_inc(qk_act, 2)
                elif name == "H1":
                    eng.wait_ge(fe_t, at(8 * n["FE8"]))
                    for k in range(2):
                        bk = full(n, k)
                        eng.activation(HE[:, 0, k * 512:k * 512 + 512], bk[:, :], ACT.Relu)\
                            .then_inc(side_free[k], 1)
                    for k in range(2):
                        eng.wait_ge(side_free[k], at(n[f"bank{k}"] + 1))
                        eng.sem_inc(hid_ready, 1)
                    eng.sem_inc(xt_used, 1)
                elif name in ("L0", "L1"):
                    ll = int(name[1])
                    if ll == 0:
                        eng.wait_ge(wc_ready, at(b + 1))
                    for k in range(2):
                        bk = full(n, k)
                        if ll == 1 and k == 0:
                            full(n, 1)
                        for g in (2 * k, 2 * k + 1):
                            c = (g % 2) * 256
                            dst = HE[:, 1, g * 256:g * 256 + 256].rearrange("p (j q) -> p j q", j=JT) \
                                if ll == 0 else \
                                HE[:, 0, :].rearrange("p (j g q) -> p j g q", j=JT, g=G)[:, :, g, :]
                            ins = eng.activation(dst, bk[:, c:c + 256].rearrange("p (j q) -> p j q", j=JT),
                                                 ACT.Relu, bias=WC[:, g, ll, HID:HID + 1])
                        ins.then_inc(side_free[k], 1)
                    for k in range(2):
                        eng.wait_ge(side_free[k], at(n[f"bank{k}"] + 1))
                        eng.sem_inc(hid_ready, 1)
                elif name == "MT":
                    eng.wait_ge(fe_t, at(8 * b))
                    eng.wait_ge(y_init, at(b))
                    for k in range(2):
                        bk = full(n, k)
                        c = k * 512
                        eng.activation(MTf[0:E, c:c + 512], bk[0:E, :], ACT.Copy).then_inc(mt_ready, 1)
                        eng.activation(MTb[0:E, c:c + 512], bk[0:E, :], ACT.Copy).then_inc(side_free[k], 1)
                    for k in range(2):
                        eng.wait_ge(side_free[k], at(n[f"bank{k}"] + 1))
                    eng.sem_inc(mt_ready, 2)
                elif name.startswith("FE") and name != "FE8":
                    e = int(name[2:])
                    eng.wait_ge(fe_t, at(8 * b + max(e - 1, 0)))
                    if e == 0:
                        eng.wait_ge(h1n_ready, at(n["WO"]))
                    bk = full(n, 0)
                    eng.activation(mbs[:, e % 2, :], bk[:, :], ACT.Copy).then_inc(side_free[0], 1)
                    eng.wait_ge(side_free[0], at(n["bank0"] + 1))
                    eng.sem_inc(mb_ready, 1)
                elif name.startswith("FW"):
                    e = int(name[2:])
                    for k in range(2):
                        bk = full(n, k)
                        eng.activation(HE[:, e % 2, k * 512:k * 512 + 512], bk[:, :], ACT.Gelu)\
                            .then_inc(side_free[k], 1)
                    for k in range(2):
                        eng.wait_ge(side_free[k], at(n[f"bank{k}"] + 1))
                    eng.sem_inc(he_ready, 2)
                    if e == E - 1:
                        eng.sem_inc(xt_used, 1)

            def acc_out(u, si):
                acc = ACC_LAST[u]
                if acc == 0:
                    eng.wait_ge(tail_d, at(4 * si))
                g, half = acc // 2, acc % 2
                eng.wait_ge(pv_done, at(TILES * (UNITS * si + u + 1)))
                eng.activation(acc_sb[:, g, half * 512:half * 512 + 512], ACC[acc % 2][:, :], ACT.Copy)\
                    .then_inc(acc_free, 1)

            def body(kind, it, v0, grp, side, found):
                if kind == "serial":
                    for n, stage in enumerate(side):
                        side_stage(stage, found[0, n])
                    return
                steps, starts, ends = boundaries(kind, grp, v0, it)
                si0 = Lin(v0.k // UNITS, v0.c // UNITS) if isinstance(v0, Lin) else v0 // UNITS
                for s in range(steps):
                    for t in range(TILES):
                        m = TILES * (v0 + s) + t
                        eng.wait_ge(st_ready, at(m + 1))
                        eng.wait_ge(pv_done, at(m - 3))
                        eng.activation(prob[:, t % 4, :], ST[t % 2][:, :], ACT.Exp).then_inc(exp_done, 1)
                        if t == 3:
                            if s > 0 and (s - 1) % UNITS in ACC_LAST:
                                acc_out((s - 1) % UNITS, si0 + (s - 1) // UNITS)
                            elif s == 0 and not starts:
                                acc_out(UNITS - 1, si0 - 1)
                        if t in (4, 7):
                            part = s + (t == 7) / 2
                            for n, stage in enumerate(side[part]):
                                side_stage(stage, found[part, n])
                if ends:
                    acc_out(UNITS - 1, si0 + (steps - 1) // UNITS)

            run_phases(eng, reg, body)

        @block.vector
        def _(eng):
            reg = [None]
            at = counter(reg)
            done = [0]

            def step(ins):
                ins.then_inc(s_dve, 1)
                done[0] += 1
                eng.wait_ge(s_dve, done[0])

            for tile in (QA[0], KA[0]):
                ins = eng.memset(tile[64:K_ALL, :, :], 0.0)
            step(ins)
            step(eng.memset(KA[0][K_MAX:K_ALL, :, :], 1.0))
            eng.wait_ge(s_dma, N_SET_DMA[0])
            eng.wait_ge(s_pe, 2)
            for part in range(2):
                for hh in range(2):
                    src = SIDE[part][64 * hh:64 * hh + 64, :].rearrange("c (o a p) -> c a o p", a=2, p=8)
                    for a in range(2):
                        ins = eng.tensor_copy(
                            Wf[64 * hh:64 * hh + 64, :, a, 32 * part:32 * part + 32].rearrange("c j o -> c o j"),
                            src[:, a, :, 4 * hh:4 * hh + 4])
            step(ins)
            eng.tensor_copy(h0c[0:2 * WINDOW, :, :].rearrange("p j c -> p (j c)").bitcast(BF16),
                            prob[0:2 * WINDOW, 0:2, :].rearrange("p a c -> p (a c)"))
            eng.tensor_copy(ident_b[:, :], ident)
            step(eng.tensor_copy(SEL[:, :, :].rearrange("p e c -> p (e c)"),
                                 CT[:, 4 * P + 200:4 * P + 200 + 512]))
            eng.wait_ge(s_pe, 4)
            biasf = QF[0:WINDOW, :]
            for a in range(2):
                ins = eng.tensor_copy(biasf[:, a * 512:a * 512 + 512], NAT[a][0:WINDOW, :])
            step(ins)
            step(eng.tensor_copy(PT[0:WINDOW, 0, :], biasf))
            step(eng.tensor_tensor(biasf, biasf, PT[0:WINDOW, 0, :], ALU.subtract))
            step(eng.tensor_copy(PT[0:WINDOW, 1, :], biasf))
            step(eng.tensor_tensor(PT[0:WINDOW, 2, :], biasf, PT[0:WINDOW, 1, :], ALU.subtract))
            for ll in range(2):
                ins = eng.tensor_tensor(WS[:, ll, 0:HID], WS[:, ll, 0:HID], ident, ALU.add)
            step(ins)
            step(eng.memset(mpart[:, :, :, :], 0.0))
            step(eng.memset(XT[64:P, :], 0.0))
            assert done[0] == SET_DVE, done[0]
            eng.wait_ge(s_pool, SET_POOL)
            eng.wait_ge(s_dma, N_SET_DMA[1])

            def full(n, k, use=0):
                eng.wait_ge(side_full[k], at(n[f"bank{k}"] + use + 1))
                return SIDE[k]

            def nat3(bk):
                return bk[:, :].rearrange("p (j c) -> p j c", j=JT)

            def side_stage(stage, n):
                name, b = stage[:2]
                if name == "TOKC":
                    eng.wait_ge(ho0, at(b))
                    bk = full(n, 0)
                    eng.tensor_copy(h0n[:, :, :], nat3(bk)).then_inc(side_free[0], 1)
                    eng.wait_ge(side_free[0], at(n["bank0"] + 1))
                    eng.sem_inc(h0n_ready, 1)
                elif name == "LN1":
                    src = {"0": h0n, "a": h0c, "1": h1n, "m": h1c}[stage[2]]
                    k = n["LN1"]
                    eng.wait_ge(ln_p, at(6 * k))
                    if stage[2] == "0":
                        eng.wait_ge(h0n_ready, at(b + 1))
                    elif stage[2] == "1":
                        eng.wait_ge(h1n_ready, at(b + 1))
                    else:
                        eng.wait_ge(hres, at(n["PROJ"]))
                    eng.tensor_reduce(ln_s[:, 0, :], src[:, :, :], AX.X, ALU.add).then_inc(ln_d, 1)
                elif name == "LN2":
                    eng.wait_ge(ln_p, at(6 * n["LN2"] + 3))
                    eng.tensor_reduce(ln_s[:, 2, :], sq[:, :, :], AX.X, ALU.add).then_inc(ln_d, 1)
                elif name == "QV":
                    eng.wait_ge(vc_done, at(n["QV"]))
                    bk = full(n, 0)
                    eng.tensor_copy(Vn[:, :, :], nat3(bk)).then_inc(side_free[0], 1)
                    eng.wait_ge(side_free[0], at(n["bank0"] + 1))
                    eng.sem_inc(vn_ready, 1)
                    eng.sem_inc(xt_used, 1)
                elif name == "COMB":
                    k4 = 4 * n["COMB"]
                    eng.wait_ge(hres, at(n["COMB"]))
                    for k in range(2):
                        bk = full(n, k)
                        eng.wait_ge(tail_d, at(k4 + 2 * k))
                        eng.reciprocal(rec[:, :], bk[64:P, :]).then_inc(tail_d, 1)
                        eng.wait_ge(tail_d, at(k4 + 2 * k + 1))
                        eng.tensor_tensor(OT[0:64, k * 512:k * 512 + 512], bk[0:64, :], rec[:, :], ALU.mult)\
                            .then_inc(side_free[k], 1)
                        eng.wait_ge(side_free[k], at(n[f"bank{k}"] + 1))
                        eng.sem_inc(tail_d, 1)
                elif name == "PROJ":
                    h, turn = (h0c, ho0) if stage[2] == 0 else (h1c, ho1)
                    eng.wait_ge(turn, at(b + 1))
                    bk = full(n, 0)
                    eng.tensor_tensor(h[:, :, :], nat3(bk), h[:, :, :], ALU.add).then_inc(side_free[0], 1)
                    eng.wait_ge(side_free[0], at(n["bank0"] + 1))
                    eng.sem_inc(hres, 1)
                elif name == "WO":
                    eng.wait_ge(bo_done, at(b + 1))
                    eng.wait_ge(ho1, at(b))
                    bk = full(n, 0)
                    eng.tensor_tensor(h1n[:, :, :], nat3(bk), h0c[:, :, :], ALU.add).then_inc(side_free[0], 1)
                    eng.wait_ge(side_free[0], at(n["bank0"] + 1))
                    eng.sem_inc(h1n_ready, 1)
                elif name == "GATE":
                    eng.wait_ge(xt_ready, at(2 * n["TR"]))
                    bk = full(n, 0)
                    eng.tensor_copy(gs[:, :, :].rearrange("p j e -> p (j e)"), bk[:, 0:JT * E])\
                        .then_inc(side_free[0], 1)
                    eng.wait_ge(side_free[0], at(n["bank0"] + 1))
                    eng.sem_inc(gate_d, 1)
                    other = gs[:, :, :].unsqueeze(2).to_broadcast([P, JT, E, E])
                    own = gs[:, :, :].unsqueeze(3).to_broadcast([P, JT, E, E])
                    for tile, op in ((xc, ALU.is_ge), (sq, ALU.is_gt)):
                        eng.tensor_tensor(tile[:, :, :].rearrange("p j (e f) -> p j e f", e=E),
                                          other, own, op).then_inc(gate_d, 1)
                elif name == "RANK":
                    eng.wait_ge(gate_p, at(3 * (b + 1)))
                    eng.tensor_reduce(rank[:, :, :], xc[:, :, :].rearrange("p j (e f) -> p j e f", e=E),
                                      AX.X, ALU.add).then_inc(gate_d, 1)
                    eng.wait_ge(gate_d, at(5 * b + 4))
                    eng.tensor_scalar(mask[:, :, :], rank[:, :, :], 1.5, None, ALU.is_lt).then_inc(gate_d, 1)
                elif name.startswith("FE"):
                    e = int(name[2:])
                    bk = full(n, 1)
                    if e == 0:
                        eng.wait_ge(out_ready, at(b))
                        eng.tensor_copy(yacc[:, :], bk[:, :]).then_inc(side_free[1], 1)
                        eng.wait_ge(side_free[1], at(n["bank1"] + 1))
                        eng.sem_inc(y_init, 1)
                        return
                    eng.wait_ge(mb_ready, at(8 * b + e))
                    eng.wait_ge(y_add, at(8 * b + max(e - 2, 0)))
                    eng.tensor_tensor(ytmp[:, (e - 1) % 2, :], bk[:, :], mbs[:, (e - 1) % 2, :], ALU.mult)\
                        .then_inc(side_free[1], 1)
                    eng.wait_ge(side_free[1], at(n["bank1"] + 1))
                    eng.sem_inc(fe_t, 1)
                elif name == "OUT":
                    eng.wait_ge(out_dma, at(16 * b))
                    bk = full(n, 0)
                    for hf in range(2):
                        ins = eng.tensor_tensor(
                            ot[:, 4 * hf:4 * hf + 4, :],
                            bk[:, :].rearrange("p (j f d) -> p f j d", j=4, f=2)[:, hf],
                            h1c[:, 4 * hf:4 * hf + 4, :], ALU.add)
                    ins.then_inc(side_free[0], 1)
                    eng.wait_ge(side_free[0], at(n["bank0"] + 1))
                    eng.sem_inc(out_ready, 1)

            def rows_out(v0, grp, s, dma_seen, last=False):
                idx = RING_USES * v0 + (RING_USES * s + 2 * grp if not last else RING_USES * (s - 1) + 2 * grp + 1)
                par = (RING_USES * s if not last else RING_USES * (s - 1) + 1) % 2
                half = Lin(v0.k // 2, v0.c // 2) if isinstance(v0, Lin) else v0 // 2
                eng.wait_ge(maxrow_in[s % 2], at(64 * (half + dma_seen)))
                eng.wait_ge(nat_ready, at(idx + 1))
                eng.tensor_copy(mrow[:, s % 2, :], NAT[par][0:4 * PARTS, 0:P]).then_inc(nat_free, 1)
                eng.wait_ge(nat_free, at(idx + 1))
                eng.sem_inc(mrow_ready, 1)

            def reduce_tile(v0, grp, s, k):
                use = RING_USES * s + 2 * grp + 1 + k
                eng.wait_ge(nat_ready, at(RING_USES * v0 + use + 1))
                if k == 0:
                    eng.wait_ge(negm_ready, at(v0 + s - 1))
                eng.tensor_reduce(mx[:, s % 2, k // 2, k % 2:k % 2 + 1], NAT[use % 2][:, :], AX.X, ALU.max)\
                    .then_inc(nat_free, 1)

            def unit_max(v0, grp, s):
                eng.wait_ge(nat_free, at(RING_USES * v0 + RING_USES * s + 2 * grp + 1 + TILES))
                eng.wait_ge(parts_ready, at(v0 + s - 1))
                eng.tensor_reduce(neg_max[:, s % 2, :], mx[:, s % 2, :, :], AX.X, ALU.max, negate=True)\
                    .then_inc(negm_ready, 1)

            def body(kind, it, v0, grp, side, found):
                if kind == "serial":
                    for n, stage in enumerate(side):
                        side_stage(stage, found[0, n])
                    return
                steps, starts, ends = boundaries(kind, grp, v0, it)
                if starts:
                    for s in range(3):
                        rows_out(v0, grp, s, 0)
                        for k in range(TILES):
                            reduce_tile(v0, grp, s, k)
                        unit_max(v0, grp, s)
                for s in range(steps):
                    ahead = s + 3
                    if not (ends and s + 1 >= steps):
                        rows_out(v0, grp, ahead, ahead // 2 - 1, last=(ends and s + 2 == steps))
                    for k in range(TILES):
                        if not (ends and ahead >= steps):
                            reduce_tile(v0, grp, ahead, k)
                        if k in (4, 7):
                            part = s + (k == 7) / 2
                            for n, stage in enumerate(side[part]):
                                side_stage(stage, found[part, n])
                    if not (ends and ahead >= steps):
                        unit_max(v0, grp, ahead)

            run_phases(eng, reg, body)

        @block.gpsimd
        def _(eng):
            reg = [None]
            at = counter(reg)

            def alone(_):
                eng.sem_inc(pool_passed, 1)

            n_set = [0]

            def clear(ap, value=0.0):
                eng.memset(ap, value).then_inc(s_pool, 1)
                n_set[0] += 1
                eng.wait_ge(s_pool, n_set[0])

            clear(QA[1][64:K_ALL, :, :])
            clear(KA[1][64:K_MAX, :, :])
            clear(KA[1][K_MAX:K_ALL, :, :], 1.0)
            for a in (0, 1):
                clear(VZ[a][:, :, :, :])
            clear(MTf[:, :])
            clear(MTb[:, :])
            clear(OT[64:P, :])
            eng.wait_ge(s_dve, SET_DVE)
            clear(XT[64:65, :], 1.0)
            clear(OT[64:65, :], 1.0)
            for a in (0, 1):
                for pos in range(3):
                    heads = [hs[pos] for hs in HEAD_GROUPS if pos < len(hs)]
                    c = ROWS_H * pos + HD
                    ins = eng.memset(VZ[a][:, :, heads[0]:heads[-1] + 1:3, c:c + 1], 1.0)
            ins.then_inc(s_pool, 1)
            eng.wait_ge(s_pool, SET_POOL)
            eng.wait_ge(s_dma, N_SET_DMA[1])

            def wide(col):
                return ln_s[:, col, :].unsqueeze(2).to_broadcast([P, JT, 64])

            def side_stage(stage, n, v0):
                name, b = stage[:2]
                if name == "LN1":
                    src = {"0": h0n, "a": h0c, "1": h1n, "m": h1c}[stage[2]]
                    k6 = 6 * n["LN1"]
                    alone(eng.wait_ge(ln_d, at(2 * n["LN1"] + 1)))
                    alone(eng.wait_ge(xt_ready, at(2 * n["LN1"])))
                    alone(eng.wait_ge(gate_d, at(5 * n["RANK"])))
                    eng.tensor_scalar(ln_s[:, 1, :], ln_s[:, 0, :], 1.0 / 64, 0.0, ALU.mult, ALU.add)\
                        .then_inc(ln_p, 1)
                    alone(eng.wait_ge(ln_p, at(k6 + 1)))
                    eng.tensor_tensor(xc[:, :, :], src[:, :, :], wide(1), ALU.subtract).then_inc(ln_p, 1)
                    alone(eng.wait_ge(ln_p, at(k6 + 2)))
                    eng.tensor_tensor(sq[:, :, :], xc[:, :, :], xc[:, :, :], ALU.mult).then_inc(ln_p, 1)
                elif name == "LN2":
                    k6 = 6 * n["LN2"]
                    alone(eng.wait_ge(ln_d, at(2 * n["LN2"] + 2)))
                    eng.tensor_scalar(ln_s[:, 3, :], ln_s[:, 2, :], 1.0 / 64, EPS, ALU.mult, ALU.add)\
                        .then_inc(ln_p, 1)
                    alone(eng.wait_ge(ln_p, at(k6 + 4)))
                    eng.tensor_tensor(ln_s[:, 4, :], ln_s[:, 3, :], half_pow, ALU.pow).then_inc(ln_p, 1)
                    alone(eng.wait_ge(ln_p, at(k6 + 5)))
                    eng.tensor_tensor(xc[:, :, :], xc[:, :, :], wide(4), ALU.mult).then_inc(ln_p, 1)
                elif name == "QK":
                    q = n["QK"]
                    alone(eng.wait_ge(qk_act, at(4 * (q + 1))))
                    eng.tensor_tensor(QF[:, :], QF[:, :], PT[:, 0, :], ALU.subtract).then_inc(split_p, 1)
                    alone(eng.wait_ge(split_p, at(3 * q + 1)))
                    eng.tensor_scalar(PT[:, 1, :], QF[:, :], 1.0, 0.0, ALU.mult, ALU.add).then_inc(split_p, 1)
                    alone(eng.wait_ge(split_p, at(3 * q + 2)))
                    eng.tensor_tensor(PT[:, 2, :], QF[:, :], PT[:, 1, :], ALU.subtract).then_inc(split_p, 1)
                elif name == "VC":
                    a, at_unit = stage[2:]
                    alone(eng.wait_ge(vn_ready, at(n["VC"] + 1)))
                    alone(eng.wait_ge(pv_done, at(TILES * (v0 + at_unit))))
                    vh = Vn[:, :, :].rearrange("p j (h d) -> p j h d", d=HD)
                    for pos in range(3):
                        heads = [hs[pos] for hs in HEAD_GROUPS if pos < len(hs)]
                        sl = slice(heads[0], heads[-1] + 1, 3)
                        c = ROWS_H * pos
                        ins = eng.tensor_copy(VZ[a][:, :, sl, c:c + HD], vh[:, :, sl, :])
                    ins.then_inc(vc_done, 1)
                elif name == "HO0":
                    alone(eng.wait_ge(h1n_ready, at(b)))
                    alone(eng.wait_ge(h0n_ready, at(b + 1)))
                    eng.tensor_copy(h0c[:, :, :], h0n[:, :, :]).then_inc(ho0, 1)
                elif name == "HO1":
                    alone(eng.wait_ge(out_ready, at(b)))
                    alone(eng.wait_ge(h1n_ready, at(b + 1)))
                    eng.tensor_copy(h1c[:, :, :], h1n[:, :, :]).then_inc(ho1, 1)
                elif name == "BO":
                    eng.tensor_tensor(h0c[:, :, :], h0c[:, :, :],
                                      bob[:, :].unsqueeze(1).to_broadcast([P, JT, 64]), ALU.add)\
                        .then_inc(bo_done, 1)
                elif name == "WCA":
                    alone(eng.wait_ge(wc_in, at(16 * G * (b + 1))))
                    for g in range(G):
                        ins = eng.tensor_tensor(WC[:, g, :, :], WC[:, g, :, :], WS[:, :, :], ALU.add)
                    ins.then_inc(wc_ready, 1)
                elif name == "GATE":
                    for m, (tile, tri) in enumerate(((xc, low), (sq, upp))):
                        alone(eng.wait_ge(gate_d, at(5 * b + 2 + m)))
                        eng.tensor_tensor(tile[:, :, :], tile[:, :, :],
                                          tri.unsqueeze(1).to_broadcast([P, JT, 64]), ALU.mult)\
                            .then_inc(gate_p, 1)
                    alone(eng.wait_ge(gate_p, at(3 * b + 2)))
                    eng.tensor_tensor(xc[:, :, :], xc[:, :, :], sq[:, :, :], ALU.add).then_inc(gate_p, 1)
                elif name.startswith("FE") and name != "FE0":
                    e = int(name[2:]) - 1
                    alone(eng.wait_ge(fe_t, at(8 * b + e + 1)))
                    alone(eng.wait_ge(y_add, at(8 * b + e)))
                    alone(eng.wait_ge(y_init, at(b + 1)))
                    eng.tensor_tensor(yacc[:, :], yacc[:, :], ytmp[:, e % 2, :], ALU.add).then_inc(y_add, 1)

            def split_max(v0, grp, s):
                v = v0 + s
                alone(eng.wait_ge(negm_ready, at(v + 1)))
                alone(eng.wait_ge(nat_ready, at(RING_USES * v0 + RING_USES * s + 2 * grp + 1)))
                p, nm, rs = mpart[:, s % 2], neg_max[:, s % 2, :], mres[:, s % 2, :]
                eng.tensor_scalar(p[:, :, 0], nm, 1.0, 0.0, ALU.mult, ALU.add).then_inc(mchain, 1)
                alone(eng.wait_ge(mchain, at(3 * v + 1)))
                eng.tensor_tensor(rs, nm, p[:, :, 0], ALU.subtract).then_inc(mchain, 1)
                alone(eng.wait_ge(mchain, at(3 * v + 2)))
                eng.tensor_scalar(p[:, :, 1], rs, 1.0, 0.0, ALU.mult, ALU.add).then_inc(mchain, 1)
                alone(eng.wait_ge(mchain, at(3 * v + 3)))
                eng.tensor_tensor(p[:, :, 2], rs, p[:, :, 1], ALU.subtract).then_inc(parts_ready, 1)

            def body(kind, it, v0, grp, side, found):
                if kind == "serial":
                    for n, stage in enumerate(side):
                        side_stage(stage, found[0, n], 0)
                    return
                steps, starts, ends = boundaries(kind, grp, v0, it)
                if starts:
                    for s in range(3):
                        split_max(v0, grp, s)
                for s in range(steps):
                    for part in (s, s + 0.5):
                        for n, stage in enumerate(side[part]):
                            side_stage(stage, found[part, n], v0)
                    if not (ends and s + 3 >= steps):
                        split_max(v0, grp, s + 3)

            run_phases(eng, reg, body)


def kernel(**inputs):
    import numpy as np
    import concourse.bacc as _bacc
    from concourse import mybir as _mybir
    from concourse.bass_utils import run_bass_kernel_spmd as _run

    inp = {k: np.asarray(v) for k, v in inputs.items()}
    f = np.float32

    def rows(*parts, n=P):
        m = np.concatenate([np.asarray(p, f).reshape(-1, p.shape[-1]) for p in parts])
        return np.concatenate([m, np.zeros((n - m.shape[0], m.shape[1]), f)])

    arrays = {}
    arrays["x"] = inp["x"]
    arrays["w_dft"] = inp["L0_tok_W"].reshape(64, 18, 64).transpose(1, 0, 2)
    ang = 2 * np.pi * np.outer(np.arange(9), np.arange(16)) / 16
    arrays["dft"] = np.concatenate([np.cos(ang), -np.sin(ang)]).astype(f) / f(4)
    tok = (np.arange(P)[None, :] * JT + np.arange(JT)[:, None]).ravel()
    hot = (tok[None, :] % WINDOW == np.arange(WINDOW)[:, None]).astype(f)
    arrays["onehot"] = np.concatenate([hot, hot])
    comb = np.zeros((3, P, P), f)
    for g, heads in enumerate(HEAD_GROUPS):
        for pos, h in enumerate(heads):
            for c in range(4):
                for d in range(HD):
                    comb[g, 32 * c + ROWS_H * pos + d, HD * h + d] = 1
                    comb[g, 32 * c + ROWS_H * pos + HD, 64 + HD * h + d] = 1
    e, o = np.arange(E)[:, None], np.arange(E)[None, :]
    low, upp = (o < e).astype(f).ravel(), (o > e).astype(f).ravel()
    sel = np.zeros((P, E, 64), f)
    for i in range(E):
        sel[i, i] = 1
    eye = np.eye(P, dtype=f)
    arrays["const"] = np.concatenate(
        [eye, *comb, np.tile(low, (P, 1)), np.tile(upp, (P, 1)), eye[:, 0:64] + eye[:, 64:128],
         np.full((P, 8), -0.5, f), sel.reshape(P, -1)], axis=1)
    arrays["qk_scale"] = np.concatenate([np.full((64, 1), HD ** -0.5, f), np.ones((64, 1), f)])
    qkv, qkvb, qkv1 = inp["L0_attn_qkv_w"].T, inp["L0_attn_qkv_b"][None, :], inp["L1_attn_qkv_w"].T
    arrays["qk_w"] = np.stack([rows(qkv[:, 0:128], qkvb[:, 0:128]), rows(qkv1[:, 0:128])])
    arrays["v_w"] = np.stack([rows(qkv[:, 128:], qkvb[:, 128:]), rows(qkv1[:, 128:])])
    arrays["pw"] = np.stack([rows(inp[f"L{a}_attn_proj_w"].T, inp[f"L{a}_attn_proj_b"][None, :])
                             for a in (0, 1)])
    arrays["wi"] = rows(inp["L0_ffn_Wi"].T, inp["L0_ffn_bi"][None, :])
    wr = np.concatenate([inp["L0_ffn_Wr"].transpose(1, 3, 0, 2),
                         inp["L0_ffn_br"].transpose(1, 2, 0)[..., None]], axis=3)
    arrays["routed"] = wr
    arrays["shared"] = np.concatenate([inp["L0_ffn_Ws"][:, 0].transpose(2, 0, 1),
                                       inp["L0_ffn_bs"][:, 0].T[..., None]], axis=2)
    arrays["wo"] = inp["L0_ffn_Wo"].T
    arrays["bo"] = inp["L0_ffn_bo"]
    arrays["table"] = inp["L0_attn_bias_table"]
    arrays["route"] = inp["L0_ffn_route_id"]
    arrays["wg"] = rows(inp["L1_ffn_Wg"], inp["L1_ffn_bg"][None, :])
    w1 = np.concatenate([inp["L1_ffn_W1"].transpose(1, 0, 2), inp["L1_ffn_b1"][None]])
    arrays["w1"] = np.concatenate([w1, np.zeros((P - 65, E, HID), f)])
    arrays["b2"] = rows(inp["L1_ffn_b2"])
    arrays["w2"] = inp["L1_ffn_W2"].transpose(1, 0, 2)
    arrays = {k: np.ascontiguousarray(v) for k, v in arrays.items()}

    nc = _bacc.Bacc("TRN2", target_bir_lowering=False, num_devices=1)
    aps = {k: nc.dram_tensor(f"in_{k}", v.shape, _mybir.dt.from_np(v.dtype), kind="ExternalInput").ap()
           for k, v in arrays.items()}
    result = nc.dram_tensor("out_h", (B, N_TOK, 64), F32, kind="ExternalOutput").ap()
    tower_kernel(nc, out=result, **aps)
    r = _run(nc, [{f"in_{k}": v for k, v in arrays.items()}], core_ids=[0])
    return r.results[0]["out_h"]
```

```python
from contextlib import ExitStack

import concourse.bass as bass
from concourse import mybir

F32 = mybir.dt.float32
BF16 = mybir.dt.bfloat16
I32 = mybir.dt.int32
ALU = mybir.AluOpType
ACT = mybir.ActivationFunctionType
AX = mybir.AxisListType

B, C, T, V_LEN = 16, 64, 128, 64
N_TOK = 1024
P = 128
JT = N_TOK // P
H, HD = 8, 8
HID = 128
E = 8
G = 4
EPS = 1e-5
PARTS = 3
PROD = PARTS * PARTS * HD
WINDOW = 7
K_MAX = 96
K_NAT = 96
K_ALL = K_MAX + PARTS
UNITS = 16
PV_TILES = ((-3,), (-2,), (-1,), (), (0,), (1, 2), (3,), (4,))
HEAD_GROUPS = [(0, 1, 2), (3, 4, 5), (6, 7)]
UNIT = [(h, half) for hs in HEAD_GROUPS for half in (0, 1) for h in hs]
ACC_OF, ACC_FIRST, ACC_LAST = {}, set(), {}
_u = 0
for _n, (_hs, _half) in enumerate((hs, half) for hs in HEAD_GROUPS for half in (0, 1)):
    ACC_FIRST.add(_u)
    for _ in _hs:
        ACC_OF[_u] = _n
        _u += 1
    ACC_LAST[_u - 1] = _n
N_ACC = 6
ROWS_H = HD + 1
TILES = 8
RING_USES = TILES + 1
DMA_QK = (PARTS + 1) * PARTS * 16

SIDE_BANKS = {
    "TOKA": (1, 0), "TOKB": (0,), "TOKC": (0,), "TR": (0, 1), "QK": (0, 1), "QV": (0,), "COMB": (0, 1),
    "PROJ": (0,), "H1": (0, 1), "L0": (0, 1), "L1": (0, 1), "WO": (0,), "GATE": (0,), "MT": (0, 1),
    "FE8": (1,), "OUT": (0,), **{f"{n}{e}": (0, 1) for e in range(8) for n in ("FE", "FW")},
}


class Lin:

    def __init__(self, k, c):
        self.k, self.c = k, c

    def __add__(self, n):
        return Lin(self.k + n.k, self.c + n.c) if isinstance(n, Lin) else Lin(self.k, self.c + n)

    __radd__ = __add__

    def __sub__(self, n):
        return self + (-n)

    def __mul__(self, n):
        return Lin(self.k * n, self.c * n)

    __rmul__ = __mul__


def side_parts(stages):
    for name, b, *more in stages:
        n = 8 if name == "CR" else max(len(SIDE_BANKS.get(name, ())), 1)
        for k in range(n):
            yield (name, b, k, k == n - 1, *more)


def side_schedule(r, f1, f2, f3, first=False):
    at = {(s, t): [] for s in range(2 * UNITS) for t in range(TILES)}

    def put(s, t, name, b, *more, every=2):
        for k, part in enumerate(side_parts([(name, b, *more)])):
            n = TILES * s + t + every * k
            at[n // TILES, n % TILES].append(part)

    def middle_of(b, n):
        for dn, name, *more in ((0, "COMB"), (0, "CR"), (18, "PROJ", 0), (21, "LN1", "a"),
                                (26, "LN2", "a"), (27, "BO"), (35, "TR", "a"), (40, "H1"), (45, "L0"),
                                (51, "L1"), (57, "WO"), (60, "LN1", "1"), (66, "LN2", "1"),
                                (75, "TR", "1"), (81, "QK", 1), (87, "QV", 1)):
            every = 8 if name == "COMB" else 2
            put(0, n + dn, name, b, *more, every=every)

    if first:
        middle_of(r, 4)
        put(9, 0, "HO0", r + 1)
        put(12, 4, "SCR", r, 1)
        put(12, 3, "VC", r, 1, 0)
        put(13, 2, "RL", r, 1, 0)
    else:
        put(0, 2, "SCR", r, 1)
        put(0, 3, "VC", r, 1, 0)
        put(2, 0, "RL", r, 1, 0)
    if f2:
        put(0, 4, "LX", r + 2, 0)
    if f1:
        put(1, 1, "COMB", r - 1, every=8)
        put(1, 1, "CR", r - 1)
        put(3, 3, "PROJ", r - 1, 1)
        put(3, 4, "LN1", r - 1, "m")
        put(4, 1, "LN2", r - 1, "m")
        put(5, 1, "TR", r - 1, "m")
        put(5, 6, "GATE", r - 1)
        put(6, 2, "RANK", r - 1)
        put(7, 0, "MT", r - 1)
        for e in range(E):
            put(8 + e, 3, f"FW{e}", r - 1, every=1)
            put(8 + e, 6, f"FE{e}", r - 1, every=1)
        put(8 + E, 3, f"FE{E}", r - 1)
        put(9 + E, 1, "OUT", r - 1)
    if f2:
        put(3, 3, "TOKA", r + 2)
        put(4, 0, "LX", r + 2, 1)
        put(5, 5 if first else 4, "TOKB", r + 2)
        put(10 if first else 6, 4, "TOKC", r + 2)
        put(16, 2, "LN1", r + 2, "0")
        put(17, 2, "LN2", r + 2, "0")
        put(19, 2, "TR", r + 2, "0")
        put(19, 7, "QK", r + 2, 0)
        put(20, 4, "QV", r + 2, 0)
        put(21, 6, "VC", r + 2, 0, UNITS)
        put(21, 7, "SCR", r + 2, 0)
        put(23, 0, "RL", r + 2, 0, UNITS)
        put(29, 0, "HO0", r + 2)
    if f3:
        put(12, 0, "WCL", r + 1)
        put(15, 0, "WCA", r + 1)
        middle_of(r + 1, 17 * TILES + 3)
    put(18, 6, "HO1", r)
    for parts in at.values():
        banks = [SIDE_BANKS[x[0]][x[2]] for x in parts if x[0] in SIDE_BANKS]
        assert len(banks) == len(set(banks)), parts
    return at


def program_phases():
    start = [("TOKA", 0), ("LX", 0, 1), ("TOKB", 0), ("TOKC", 0), ("LN1", 0, "0"),
             ("LN2", 0, "0"), ("TR", 0, "0"), ("QK", 0, 0), ("QV", 0, 0), ("SCR", 0, 0),
             ("VC", 0, 0, 0), ("RL", 0, 0, 0), ("HO0", 0)]
    first = {(s, t): [] for s in range(UNITS) for t in range(TILES)}
    for s, *stages in ((0, ("LX", 1, 0)), (3, ("TOKA", 1), ("LX", 1, 1)), (5, ("TOKB", 1)),
                       (6, ("TOKC", 1)), (7, ("LN1", 1, "0")), (8, ("LN2", 1, "0")),
                       (9, ("TR", 1, "0")), (10, ("QK", 1, 0), ("WCL", 0)), (11, ("QV", 1, 0)),
                       (13, ("SCR", 1, 0), ("WCA", 0))):
        for k, part in enumerate(side_parts(stages)):
            first[s, 2 * k].append(part)
    middle = [("VC", 1, 0, UNITS), ("RL", 1, 0, UNITS)]
    last = side_schedule(B - 1, True, False, False)
    tail = [x for s in range(UNITS, 2 * UNITS) for t in range(TILES) for x in last.pop((s, t))
            if x[0] != "HO1"]
    v_last = UNITS + 2 * UNITS * (B - 1)
    late = [("SCR", B - 1, 1), ("VC", B - 1, 1, v_last), ("RL", B - 1, 1, v_last)]
    for s in last:
        last[s] = [x for x in last[s] if x[0] not in ("SCR", "VC", "RL")]
    end = tail + list(side_parts([("HO1", B - 1)]))
    f1 = side_schedule(B, True, False, False)
    end += [x for s in sorted(f1) for x in f1[s] if x[0] not in ("SCR", "VC", "RL", "HO1")]
    r = Lin(1, 0)
    return [
        ("serial", None, 0, 0, list(side_parts(start))),
        ("units", (0, 0), 0, 0, first),
        ("serial", None, UNITS, 1, list(side_parts(middle))),
        ("pair", 0, UNITS, 1, side_schedule(0, False, True, True, True)),
        ("pair", 1, 3 * UNITS, 1, side_schedule(1, True, True, True)),
        ("loop", r, Lin(2 * UNITS, UNITS), 1, side_schedule(r, True, True, True)),
        ("pair", B - 2, UNITS + 2 * UNITS * (B - 2), 1, side_schedule(B - 2, True, False, True)),
        ("serial", None, v_last, 2, list(side_parts(late))),
        ("units", (1, B - 1), v_last, 2, last),
        ("serial", None, v_last + UNITS, 2, end),
    ]


LOOP_FROM, LOOP_TO = 2, B - 2


def side_counts(side, before):
    found, now = {}, dict(before)
    steps = side if isinstance(side, dict) else {(0, 0): side}
    for s in sorted(steps):
        for n, (name, _, k, is_last, *_) in enumerate(steps[s]):
            found[s, n] = dict(now)
            if is_last:
                now[name] = now.get(name, 0) + 1
            if name in SIDE_BANKS:
                bank = f"bank{SIDE_BANKS[name][k]}"
                now[bank] = now.get(bank, 0) + 1
    return found, now


NAMES = ["LX", "TOKA", "TOKB", "TOKC", "LN1", "LN2", "TR", "QK", "QV", "SCR", "VC", "RL", "HO0", "HO1",
         "COMB", "CR", "PROJ", "BO", "H1", "L0", "L1", "WO", "GATE", "RANK", "MT", "OUT", "WCL", "WCA",
         "bank0", "bank1"] + [f"{n}{e}" for e in range(9) for n in ("FE", "FW")]


def counted_phases():
    now, out = dict.fromkeys(NAMES, 0), []
    for phase in program_phases():
        side = phase[4]
        if phase[0] == "loop":
            _, after = side_counts(side, dict.fromkeys(NAMES, 0))
            before = {k: Lin(after[k], now[k] - LOOP_FROM * after[k]) for k in NAMES}
            found, _ = side_counts(side, before)
            now = {k: now[k] + (LOOP_TO - LOOP_FROM) * after[k] for k in NAMES}
        else:
            found, now = side_counts(side, now)
        out.append((*phase, found))
    return out


def unit_of(kind, it, s):
    if kind == "units":
        return it[0], it[1], s
    if s < UNITS:
        return 0, it + 1, s
    if s < 2 * UNITS:
        return 1, it, s - UNITS
    return 0, it + 2, s - 2 * UNITS


def tower_kernel(nc, x, w_dft, dft, const, onehot, qk_w, v_w, pw, qk_scale, wi, routed, shared, wo, bo,
                 table, route, wg, w1, b2, w2, out):
    with ExitStack() as ctx:
        def sb(name, shape, dt=F32):
            return ctx.enter_context(nc.sbuf_tensor(name, shape, dt))

        def bank(name):
            return ctx.enter_context(nc.psum_tensor(name, [P, 512], F32))

        def sem(name):
            return ctx.enter_context(nc.semaphore(name))

        QA = [sb(f"q_rows{a}", [K_ALL, H, N_TOK], BF16) for a in (0, 1)]
        KA = [sb(f"k_rows{a}", [K_ALL, H, N_TOK], BF16) for a in (0, 1)]
        VZ = [sb(f"v_padded{a}", [P, JT, H, 32]) for a in (0, 1)]
        prob = sb("prob", [P, TILES, 512])
        mx = sb("tile_max", [P, 2, 4, 2])
        neg_max = sb("neg_max", [P, 2, 4])
        mres = sb("max_residue", [P, 2, 4])
        mpart = sb("max_parts", [P, 2, PARTS, 4], BF16)
        mrow = sb("max_rows", [4 * PARTS, 2, P], BF16)
        acc_sb = sb("acc_sb", [P, 3, N_TOK])
        xt = sb("x_rows", [P, 8, 256])
        xe = sb("x_edge", [P, V_LEN])
        AB = sb("patch_halves", [P, N_TOK])
        h0n, h0c, h1n, h1c = (sb(n, [P, JT, 64]) for n in ("h0n", "h0c", "h1n", "h1c"))
        xc, sq = sb("centred", [P, JT, 64]), sb("squares", [P, JT, 64])
        ln_s = sb("ln_s", [P, 5, JT])
        XT = sb("ln_rows", [P, N_TOK])
        QF = sb("qk_f32", [P, N_TOK])
        PT = sb("qk_parts", [P, PARTS, N_TOK], BF16)
        Vn = sb("v_natural", [P, JT, 64])
        rec = sb("reciprocals", [64, 512])
        OT = sb("attn_rows", [P, N_TOK])
        WC = sb("group_weights", [P, G, 2, HID + 1])
        WS = sb("shared_weights", [P, 2, HID + 1])
        HE = sb("hidden", [P, 2, N_TOK])
        mbs = sb("mask_rows", [P, 2, 512])
        ytmp = sb("y_masked", [P, 2, 512])
        yacc = sb("y_sum", [P, 512])
        gs = sb("gate_scores", [P, JT, E])
        rank = sb("gate_rank", [P, JT, E])
        mask = sb("top2_mask", [P, JT, E])
        MTf = sb("mask_t", [P, N_TOK])
        MTb = sb("mask_tb", [P, N_TOK], BF16)
        ot = sb("out_rows", [P, JT, 64])
        n_const = const.shape[1]
        CT = sb("const", [P, n_const])
        ident, comb = CT[:, 0:P], [CT[:, P * (g + 1):P * (g + 2)] for g in range(3)]
        at = 4 * P
        low, upp = CT[:, at:at + 64], CT[:, at + 64:at + 128]
        fold = CT[:, at + 128:at + 192]
        half_pow = CT[:, at + 192:at + 200]
        ident_b = sb("ident_b", [P, P], BF16)
        SEL = sb("expert_rows", [P, E, 64], BF16)
        Wf = sb("w_patch", [P, 4, 2, 64])
        WQK = [sb(f"w_qk{a}", [P, P]) for a in (0, 1)]
        WV = [sb(f"w_v{a}", [P, 64]) for a in (0, 1)]
        WP = [sb(f"w_proj{a}", [P, 64]) for a in (0, 1)]
        scl = sb("qk_scale", [P, 1])
        WI = sb("w_in", [P, HID])
        WO = sb("w_out", [P, 64])
        bob = sb("b_out", [P, 64])
        WG = sb("w_gate", [P, E])
        W1 = sb("w_1", [P, E, HID])
        W2 = sb("w_2", [P, E, 64])
        B2 = sb("b_2", [P, 64])
        dftc = sb("dft", [18, 16])
        T3 = sb("bias_table", [WINDOW, WINDOW])
        routes = sb("routes", [1, B * G], I32)
        scr = [nc.dram_tensor(f"q_scratch{a}", (PARTS, 64, N_TOK), BF16, kind="Internal").ap()
               for a in (0, 1)]
        scr_k = [nc.dram_tensor(f"k_scratch{a}", (H, PARTS, HD, N_TOK), BF16, kind="Internal").ap()
                 for a in (0, 1)]

        NAT = [bank("nat0"), bank("nat1"), bank("nat2")]
        ST = [bank("st0"), bank("st1")]
        ACC = bank("acc")
        SIDE = [bank("side0"), bank("side1")]

        s_dft = sem("dft_in")
        s_dma, s_dve, s_pool, s_pe, s_act = (sem(n) for n in
                                             ("set_dma", "set_dve", "set_pool", "set_pe", "set_act"))
        nat_ready, nat_free, negm_ready = sem("nat_ready"), sem("nat_free"), sem("negm_ready")
        mchain, parts_ready, mrow_ready = sem("mchain"), sem("parts_ready"), sem("mrow_ready")
        maxrow_in = [sem("maxrow_in0"), sem("maxrow_in1")]
        st_ready, exp_done, pv_done = sem("st_ready"), sem("exp_done"), sem("pv_done")
        acc_free = sem("acc_free")
        side_full = [sem("side_full0"), sem("side_full1")]
        side_free = [sem("side_free0"), sem("side_free1")]
        x_in, x_used, edge_in, ab_ready = sem("x_in"), sem("x_used"), sem("edge_in"), sem("ab_ready")
        h0n_ready, h1n_ready, ho0, ho1 = sem("h0n_ready"), sem("h1n_ready"), sem("ho0"), sem("ho1")
        ln_d, ln_p, xt_ready, xt_used = sem("ln_d"), sem("ln_p"), sem("xt_ready"), sem("xt_used")
        qk_act, split_p, vn_ready, vc_done = sem("qk_act"), sem("split_p"), sem("vn_ready"), sem("vc_done")
        scr_out = sem("scr_out")
        qk_in = [sem("qk_in0"), sem("qk_in1")]
        tail_d, hres = sem("tail_d"), sem("hres")
        bo_done, hid_ready, wc_in, wc_ready = sem("bo_done"), sem("hid_ready"), sem("wc_in"), sem("wc_ready")
        gate_d, gate_p, mt_ready = sem("gate_d"), sem("gate_p"), sem("mt_ready")
        he_ready, mb_ready, fe_t, y_init, y_add = (sem(n) for n in
                                                  ("he_ready", "mb_ready", "fe_t", "y_init", "y_add"))
        out_ready, out_dma = sem("out_ready"), sem("out_dma")

        sp_passed, pe_passed, pool_passed = sem("sp_passed"), sem("pe_passed"), sem("pool_passed")

        PHASES = counted_phases()
        block = ctx.enter_context(nc.Block())

        def counter(reg):
            def at(n):
                if isinstance(n, Lin):
                    if n.k:
                        assert n.k * LOOP_FROM + n.c > 0 and n.k > 0, (n.k, n.c)
                        return reg[0] * n.k + n.c
                    n = n.c
                return max(n, 0)
            return at

        def run_phases(eng, reg, body):
            for kind, it, v0, grp, side, found in PHASES:
                if kind == "loop":
                    with eng.Fori(LOOP_FROM, LOOP_TO) as r:
                        reg[0] = r
                        body("pair", it, v0, grp, side, found)
                else:
                    body(kind, it, v0, grp, side, found)

        def boundaries(kind, grp, v0, it):
            steps = UNITS if kind == "units" else 2 * UNITS
            starts = kind == "units" or it == 0 and not isinstance(it, Lin)
            ends = kind == "units" or (not isinstance(it, Lin) and it == B - 2)
            return steps, starts, ends

        def vc_index(a, b):
            if a == 1:
                return 2 * b + 3 if isinstance(b, Lin) or b < B - 1 else 2 * b + 2
            return 2 * b if isinstance(b, Lin) or b > 0 else 1

        N_SET_DMA = [0]
        SET_DVE, SET_POOL, SET_PE, SET_ACT = 12, 11, 2, 0

        @block.sync
        def _(eng):
            reg = [None]
            at = counter(reg)

            def alone(_):
                eng.sem_inc(sp_passed, 1)

            n_dma = [0]

            def load(dst, src, done=s_dma):
                eng.dma_start(dst, src).then_inc(done, 16)
                n_dma[0] += 16 if done is s_dma else 0

            def load_x(b, half):
                item = x[b if isinstance(b, int) else reg[0] * b.k + b.c]
                for hh in range(2):
                    eng.dma_start(xt[64 * hh:64 * hh + 64, :, :],
                                  item.rearrange("c (m h j) v -> c m h (j v)", h=2, j=4)
                                  [:, 8 * half:8 * half + 8, hh]).then_inc(x_in, 16)
                if half == 0:
                    for hh in range(2):
                        eng.dma_start(xe[64 * hh:64 * hh + 64, :], item[:, T - 1, :]).then_inc(edge_in, 16)

            load(dftc[:, :], dft, s_dft)
            load(acc_sb[0:18, 0:2, :], w_dft[:, 0:32].rearrange("f (a o) c -> f a (o c)", a=2), s_dft)
            load(HE[0:18, :, :], w_dft[:, 32:64].rearrange("f (a o) c -> f a (o c)", a=2), s_dft)
            load_x(0, 0)
            load(CT[:, :], const)
            load(prob[0:2 * WINDOW, 0:2, :], onehot.rearrange("r (a c) -> r a c", a=2))
            for c7 in range(WINDOW):
                load(T3[c7:c7 + 1, :], table[WINDOW - 1 - c7:2 * WINDOW - 1 - c7].unsqueeze(0))
            load(scl[:, :], qk_scale)
            load(WI[:, :], wi)
            load(WO[:, :], wo)
            load(bob[:, :], bo.unsqueeze(0).to_broadcast([P, 64]))
            load(WS[:, :, :], shared)
            load(WG[:, :], wg)
            load(W1[:, :, :], w1)
            load(W2[:, :, :], w2)
            load(B2[:, :], b2)
            for a in (0, 1):
                load(WQK[a][:, :], qk_w[a])
                load(WV[a][:, :], v_w[a])
                load(WP[a][:, :], pw[a])
            load(routes[:, :], route.unsqueeze(0))
            N_SET_DMA[0] = n_dma[0]
            eng.wait_ge(s_dve, SET_DVE)
            eng.wait_ge(s_pool, SET_POOL)
            hot = h0c[0:2 * WINDOW, :, :].rearrange("p j c -> p (j c)").bitcast(BF16)
            for s in range(PARTS):
                row = PROD + WINDOW * s
                load(QA[0][row:row + WINDOW, :, :], hot[0:WINDOW, :].unsqueeze(1).to_broadcast([WINDOW, H, N_TOK]))
                load(KA[0][row:row + WINDOW, :, :],
                     PT[0:WINDOW, s, :].unsqueeze(1).to_broadcast([WINDOW, H, N_TOK]))
            N_SET_DMA.append(n_dma[0])
            eng.wait_ge(s_dma, n_dma[0])

            def max_dma(kind, it, v0, s):
                a, b, u = unit_of(kind, it, s)
                h, half = UNIT[u]
                eng.dma_start(QA[a][K_MAX:K_ALL, h, half * 512:half * 512 + 512],
                              mrow[:, s % 2, :]).then_inc(maxrow_in[s % 2], 16)

            def side_stage(stage, n, v0):
                name, b, _, _, *more = stage
                if name == "LX":
                    half = more[0]
                    alone(eng.wait_ge(x_used, at(2 * b + half)))
                    load_x(b, half)
                elif name == "SCR":
                    a = more[0]
                    alone(eng.wait_ge(split_p, at(3 * (n["SCR"] + 1))))
                    alone(eng.wait_ge(qk_in[a], at(DMA_QK * b)))
                    eng.dma_start(scr[a].rearrange("i p n -> p i n"), PT[0:64, :, :]).then_inc(scr_out, 16)
                    for j in range(PARTS):
                        eng.dma_start(scr_k[a][:, j], PT[64:P, j, :]).then_inc(scr_out, 16)
                elif name == "RL":
                    a, at_unit = more
                    alone(eng.wait_ge(scr_out, at(16 * (1 + PARTS) * (n["RL"] + 1))))
                    alone(eng.wait_ge(st_ready, at(TILES * (v0 + at_unit))))
                    for i in range(PARTS):
                        rows = slice(PARTS * HD * i, PARTS * HD * (i + 1))
                        for j in range(PARTS):
                            row = PARTS * HD * i + HD * j
                            eng.dma_start(QA[a][row:row + HD, :, :],
                                          scr[a][i, 0:64, :].rearrange("(h d) n -> d h n", d=HD))\
                                .then_inc(qk_in[a], 16)
                        eng.dma_start(KA[a][rows, :, :],
                                      scr_k[a].rearrange("h j d n -> (j d) h n")).then_inc(qk_in[a], 16)
                elif name == "WCL":
                    alone(eng.wait_ge(hid_ready, at(6 * b)))
                    for g in range(G):
                        idx = b * G + g if isinstance(b, int) else reg[0] * (b.k * G) + (b.c * G + g)
                        e = eng.value_load(routes[0:1, bass.ds(idx, 1)], min_val=0, max_val=15)
                        eng.dma_start(WC[:, g, :, :], routed[bass.ds(e, 1)].squeeze(0)).then_inc(wc_in, 16)
                elif name == "OUT":
                    item = b if isinstance(b, int) else reg[0] * b.k + b.c
                    alone(eng.wait_ge(out_ready, at(b + 1)))
                    eng.dma_start(out[item].rearrange("(p j) d -> p j d", j=JT), ot[:, :, :])\
                        .then_inc(out_dma, 16)

            def body(kind, it, v0, grp, side, found):
                if kind == "serial":
                    for n, stage in enumerate(side):
                        side_stage(stage, found[(0, 0), n], v0 if stage[0] not in ("RL", "VC") else 0)
                    return
                steps, starts, ends = boundaries(kind, grp, v0, it)
                if starts:
                    alone(eng.wait_ge(mrow_ready, at(v0 + 2 + 2 * grp + 1)))
                    max_dma(kind, it, v0, 0)
                for s in range(steps):
                    if not (ends and s + 1 >= steps):
                        alone(eng.wait_ge(mrow_ready, at(v0 + (s + 1) + 2 + 2 * grp + 1)))
                        max_dma(kind, it, v0, s + 1)
                    for t in range(TILES):
                        for n, stage in enumerate(side[s, t]):
                            side_stage(stage, found[(s, t), n], v0)

            run_phases(eng, reg, body)
            alone(eng.wait_ge(out_dma, at(16 * B)))

        @block.tensor
        def _(eng):
            reg = [None]
            at = counter(reg)
            eng.wait_ge(s_dft, 48)
            for part, w in enumerate((acc_sb, HE)):
                wv = w[0:18, 0:2, :].rearrange("f a (o c) -> f a o c", c=64)
                for o in range(32):
                    for c in (0, 64):
                        mm = eng.matmul(SIDE[part][c:c + 64, o * 16:o * 16 + 16], wv[:, o // 16, o % 16, :],
                                        dftc[:, :], start=(o == 0), stop=True, skip_group_check=True)
                mm.then_inc(s_pe, 1)
            eng.wait_ge(s_dma, N_SET_DMA[0])
            for a in range(2):
                mm = eng.matmul(NAT[a][0:WINDOW, :], T3[:, :], prob[0:WINDOW, a, :], start=True, stop=True)
                mm.then_inc(s_pe, 1)
            eng.wait_ge(s_dve, SET_DVE)
            eng.wait_ge(s_pool, SET_POOL)
            eng.wait_ge(s_dma, N_SET_DMA[1])

            def side_bank(n, k, use=0, passed=None):
                eng.wait_ge(side_free[k], at(n[f"bank{k}"] + use))
                if passed is not None:
                    eng.sem_inc(passed, 1)
                return SIDE[k]

            def tok_block(n, dst, cols, rhs):
                for j in range(4):
                    mm = eng.matmul(dst[:, 0:cols], Wf[:, j, :, :].rearrange("p a o -> p (a o)"), rhs(j),
                                    start=(j == 0), stop=(j == 3))
                return mm

            def side_stage(stage, n):
                name, b, k, is_last, *more = stage
                if name in ("TOKA", "TOKB"):
                    half = name == "TOKB"
                    eng.wait_ge(x_in, at(32 * (2 * b + half + 1)))
                    if name == "TOKA" and k == 0:
                        eng.wait_ge(edge_in, at(32 * (b + 1)))
                        tok_block(n, side_bank(n, 1), 64, lambda j: xe[:, :]).then_inc(side_full[1], 1)
                        return
                    bk = side_bank(n, 0)
                    xv = xt[:, :, :].rearrange("p m (j v) -> p m j v", j=4)
                    for j in range(4):
                        mm = eng.matmul(bk[:, :], Wf[:, j, :, :].rearrange("p a o -> p (a o)"),
                                        xv[:, :, j, :], start=(j == 0), stop=(j == 3))
                    mm.then_inc(side_full[0], 1)
                elif name == "TOKC":
                    eng.wait_ge(ab_ready, at(3 * (b + 1)))
                    bk = side_bank(n, 0)
                    for j in range(JT):
                        mm = eng.matmul(bk[:, j * 64:j * 64 + 64], AB[:, j * P:j * P + P], fold,
                                        start=(j == 0), stop=True, skip_group_check=True)
                    mm.then_inc(side_full[0], 1)
                elif name == "TR":
                    eng.wait_ge(ln_p, at(6 * (n["TR"] + 1)))
                    eng.sem_inc(pe_passed, 1)
                    bk = side_bank(n, k, 0, pe_passed)
                    for j in range(4):
                        mm = eng.transpose(bk[0:64, j * P:j * P + P], xc[:, 4 * k + j, :], ident)
                    mm.then_inc(side_full[k], 1)
                elif name == "QK":
                    a = more[0]
                    eng.wait_ge(xt_ready, at(2 * n["TR"]))
                    bk = side_bank(n, k)
                    eng.matmul(bk[:, :], WQK[a][:, :], XT[:, k * 512:k * 512 + 512],
                               start=True, stop=True).then_inc(side_full[k], 1)
                elif name == "QV":
                    a = more[0]
                    bk = side_bank(n, 0)
                    for j in range(JT):
                        mm = eng.matmul(bk[:, j * 64:j * 64 + 64], XT[:, j * P:j * P + P], WV[a][:, :],
                                        start=(j == 0), stop=True, skip_group_check=True)
                    mm.then_inc(side_full[0], 1)
                elif name == "COMB":
                    eng.wait_ge(acc_free, at(N_ACC * (n["COMB"] + 1)))
                    bk = side_bank(n, k)
                    for g in range(3):
                        mm = eng.matmul(bk[:, :], comb[g], acc_sb[:, g, k * 512:k * 512 + 512],
                                        start=(g == 0), stop=(g == 2))
                    mm.then_inc(side_full[k], 1)
                elif name == "PROJ":
                    eng.wait_ge(tail_d, at(4 * (n["PROJ"] + 1)))
                    bk = side_bank(n, 0)
                    for j in range(JT):
                        mm = eng.matmul(bk[:, j * 64:j * 64 + 64], OT[:, j * P:j * P + P], WP[more[0]][:, :],
                                        start=(j == 0), stop=True, skip_group_check=True)
                    mm.then_inc(side_full[0], 1)
                elif name == "H1":
                    eng.wait_ge(xt_ready, at(2 * n["TR"]))
                    xg = XT[:, :].rearrange("p (j q) -> p j q", j=JT)
                    bk = side_bank(n, k)
                    for g in (2 * k, 2 * k + 1):
                        c = (g % 2) * 256
                        mm = eng.matmul(bk[:, c:c + 256], WI[:, :], xg[:, :, 32 * g:32 * g + 32],
                                        start=(g % 2 == 0), stop=True, skip_group_check=True)
                    mm.then_inc(side_full[k], 1)
                elif name in ("L0", "L1"):
                    ll = int(name[1])
                    eng.wait_ge(wc_ready, at(b + 1))
                    eng.wait_ge(hid_ready, at(6 * b + 2 * ll + 1 + k))
                    bk = side_bank(n, k)
                    for g in (2 * k, 2 * k + 1):
                        c = (g % 2) * 256
                        mm = eng.matmul(bk[:, c:c + 256], WC[:, g, ll, 0:HID], HE[:, ll, g * 256:g * 256 + 256],
                                        start=(g % 2 == 0), stop=True, skip_group_check=True)
                    mm.then_inc(side_full[k], 1)
                elif name == "WO":
                    eng.wait_ge(hid_ready, at(6 * (b + 1)))
                    bk = side_bank(n, 0)
                    for j in range(JT):
                        mm = eng.matmul(bk[:, j * 64:j * 64 + 64], HE[:, 0, j * P:j * P + P], WO[:, :],
                                        start=(j == 0), stop=True, skip_group_check=True)
                    mm.then_inc(side_full[0], 1)
                elif name == "GATE":
                    eng.wait_ge(xt_ready, at(2 * n["TR"]))
                    bk = side_bank(n, 0)
                    for j in range(JT):
                        mm = eng.matmul(bk[:, j * E:j * E + E], XT[:, j * P:j * P + P], WG[:, :],
                                        start=(j == 0), stop=True, skip_group_check=True)
                    mm.then_inc(side_full[0], 1)
                elif name == "MT":
                    eng.wait_ge(gate_d, at(5 * (b + 1)))
                    eng.sem_inc(pe_passed, 1)
                    bk = side_bank(n, k, 0, pe_passed)
                    for j in range(4):
                        mm = eng.transpose(bk[0:E, j * P:j * P + P], mask[:, 4 * k + j, :], ident)
                    mm.then_inc(side_full[k], 1)
                elif name.startswith("FE"):
                    e = int(name[2:])
                    if e == 0:
                        eng.wait_ge(mt_ready, at(4 * (b + 1)))
                    if not is_last:
                        bk = side_bank(n, 0)
                        for hf in range(2):
                            mm = eng.matmul(bk[64 * hf:64 * hf + 64, :], SEL[:, e, :],
                                            MTb[:, hf * 512:hf * 512 + 512], start=True, stop=True)
                        mm.then_inc(side_full[0], 1)
                        return
                    bk = side_bank(n, 1)
                    if e > 0:
                        eng.wait_ge(he_ready, at(16 * b + 2 * e))
                    for hf in range(2):
                        w, m = (B2[:, :], MTf[:, hf * 512:hf * 512 + 512]) if e == 0 else \
                            (W2[:, e - 1, :], HE[:, (e - 1) % 2, hf * 512:hf * 512 + 512])
                        mm = eng.matmul(bk[64 * hf:64 * hf + 64, :], w, m, start=True, stop=True)
                    mm.then_inc(side_full[1], 1)
                elif name.startswith("FW"):
                    e = int(name[2:])
                    bk = side_bank(n, k)
                    eng.matmul(bk[:, :], W1[:, e, :], XT[:, k * 512:k * 512 + 512],
                               start=True, stop=True).then_inc(side_full[k], 1)
                elif name == "OUT":
                    eng.wait_ge(y_add, at(8 * (b + 1)))
                    eng.sem_inc(pe_passed, 1)
                    bk = side_bank(n, 0, 0, pe_passed)
                    for j in range(4):
                        mm = eng.transpose(bk[:, j * P:j * P + P], yacc[:, j * P:j * P + P], ident)
                    mm.then_inc(side_full[0], 1)

            def parts_turn(idx, s, v):
                eng.wait_ge(nat_free, at(idx - len(NAT) + 1))
                eng.matmul(NAT[s[0]][0:4 * PARTS, 0:P], mpart[:, s[1], :, :].rearrange("p i q -> p (i q)"),
                           ident_b[:, :], start=True, stop=True).then_inc(nat_ready, 1)

            def turn_in(v0, grp, s, real, last=False):
                idx = RING_USES * v0 + (RING_USES * s + 2 * grp if not last else RING_USES * (s - 1) + 2 * grp + 1)
                place = (RING_USES * s + 2 * grp if not last else RING_USES * (s - 1) + 2 * grp + 1) % len(NAT)
                if real:
                    eng.wait_ge(parts_ready, at(v0 + s - 1))
                parts_turn(idx, (place, s % 2), None)

            def nat(kind, it, v0, grp, s, k):
                a, b, u = unit_of(kind, it, s)
                h, half = UNIT[u]
                if u == 0 and k == 0:
                    eng.wait_ge(qk_in[a], at(DMA_QK * (b + 1)))
                use = RING_USES * s + 2 * grp + 1 + k
                eng.wait_ge(nat_free, at(RING_USES * v0 + use - len(NAT) + 1))
                c, kh = half * 512 + (k // 2) * P, k % 2
                eng.matmul(NAT[use % len(NAT)][:, :], QA[a][0:K_NAT, h, c:c + P],
                           KA[a][0:K_NAT, h, kh * 512:kh * 512 + 512], start=True, stop=True)\
                    .then_inc(nat_ready, 1)

            def scores(kind, it, v0, s, t):
                a, b, u = unit_of(kind, it, s)
                h, half = UNIT[u]
                if t == 0:
                    if isinstance(v0, Lin):
                        units = Lin(v0.k // 2, v0.c // 2) + s // 2 + 1
                    else:
                        units = v0 // 2 + s // 2 + 1
                    eng.wait_ge(maxrow_in[s % 2], at(16 * units))
                eng.wait_ge(exp_done, at(TILES * (v0 + s) + t - 1))
                eng.matmul(ST[t % 2][:, :], KA[a][0:K_ALL, h, t * P:t * P + P],
                           QA[a][0:K_ALL, h, half * 512:half * 512 + 512], start=True, stop=True)\
                    .then_inc(st_ready, 1)

            def pv(a, b, u, v, si, t):
                h, half = UNIT[u]
                acc = ACC_OF[u]
                if u == 0 and t == 0:
                    eng.wait_ge(vc_done, at(vc_index(a, b)))
                eng.wait_ge(exp_done, at(TILES * v + t + 1))
                if u in ACC_FIRST and t == 0:
                    eng.wait_ge(acc_free, at(N_ACC * si + acc))
                c = 32 * (t % 4)
                mm = eng.matmul(ACC[c:c + 32, :], VZ[a][:, t, h, :], prob[:, t, :],
                                start=(u in ACC_FIRST and t < 4), stop=(u in ACC_LAST and t >= 4),
                                skip_group_check=True)
                mm.then_inc(pv_done, 1)

            def body(kind, it, v0, grp, side, found):
                if kind == "serial":
                    for n, stage in enumerate(side):
                        side_stage(stage, found[(0, 0), n])
                    return
                steps, starts, ends = boundaries(kind, grp, v0, it)
                si0 = Lin(v0.k // UNITS, v0.c // UNITS) if isinstance(v0, Lin) else v0 // UNITS
                if starts:
                    for s in range(3):
                        turn_in(v0, grp, s, s == 2)
                        for k in range(TILES):
                            nat(kind, it, v0, grp, s, k)

                def pv_at(s, t):
                    if s < 0:
                        if not starts:
                            pv(1, it - 1, UNITS - 1, v0 - 1, si0 - 1, t)
                        return
                    a, b, u = unit_of(kind, it, s)
                    pv(a, b, u, v0 + s, si0 + s // UNITS, t)

                for s in range(steps):
                    ahead = s + 3
                    has_nat = not (ends and ahead >= steps)
                    if not (ends and s + 1 >= steps):
                        turn_in(v0, grp, ahead, True, last=(ends and s + 2 == steps))
                    for t in range(TILES):
                        for n, stage in enumerate(side[s, t]):
                            side_stage(stage, found[(s, t), n])
                        if has_nat:
                            nat(kind, it, v0, grp, ahead, t)
                        scores(kind, it, v0, s, t)
                        for tile in PV_TILES[t]:
                            pv_at(s + tile // TILES, tile % TILES)
                if ends:
                    for t in range(PV_TILES[0][0] + TILES, TILES):
                        pv_at(steps - 1, t)

            run_phases(eng, reg, body)

        @block.scalar
        def _(eng):
            reg = [None]
            at = counter(reg)
            eng.wait_ge(s_dve, SET_DVE)
            eng.wait_ge(s_pool, SET_POOL)
            eng.wait_ge(s_dma, N_SET_DMA[1])

            def full(n, k, use=0):
                eng.wait_ge(side_full[k], at(n[f"bank{k}"] + use + 1))
                return SIDE[k]

            by_patch = AB[:, :].rearrange("p (j v n) -> p j v n", j=JT, n=2)

            def half_patches(bk, half):
                v = bk[:, :].rearrange("p (m v) -> p m v", m=8)
                eng.activation(by_patch[0:64, :, :, half], v[0:64], ACT.Copy)
                if half == 1:
                    eng.activation(by_patch[64:P, JT - 1, :, 0], v[64:P, 0, :], ACT.Copy)
                return eng.activation(by_patch[64:P, 0:JT - 1, :, half], v[64:P, 1:8, :], ACT.Copy)

            def side_stage(stage, n):
                name, b, k, is_last, *more = stage
                if name == "TOKA" and k == 0:
                    eng.wait_ge(h0n_ready, at(b))
                    bk = full(n, 1)
                    eng.activation(by_patch[64:P, JT - 1, :, 1], bk[64:P, 0:64], ACT.Copy)\
                        .then_inc(side_free[1], 1)
                    eng.wait_ge(side_free[1], at(n["bank1"] + 1))
                    eng.sem_inc(ab_ready, 1)
                elif name == "TOKA":
                    half_patches(full(n, 0), 0).then_inc(side_free[0], 1)
                    eng.wait_ge(side_free[0], at(n["bank0"] + 1))
                    eng.sem_inc(ab_ready, 1)
                    eng.sem_inc(x_used, 1)
                elif name == "TOKB":
                    half_patches(full(n, 0), 1).then_inc(side_free[0], 1)
                    eng.wait_ge(side_free[0], at(n["bank0"] + 1))
                    eng.sem_inc(ab_ready, 1)
                    eng.sem_inc(x_used, 1)
                elif name == "TR":
                    eng.wait_ge(xt_used, at(n["TR"]))
                    bk = full(n, k)
                    eng.activation(XT[0:64, k * 512:k * 512 + 512], bk[0:64, :], ACT.Copy)\
                        .then_inc(side_free[k], 1)
                    eng.wait_ge(side_free[k], at(n[f"bank{k}"] + 1))
                    eng.sem_inc(xt_ready, 1)
                elif name == "QK":
                    eng.wait_ge(split_p, at(3 * n["QK"]))
                    eng.wait_ge(scr_out, at(16 * (1 + PARTS) * n["QK"]))
                    bk = full(n, k)
                    c = k * 512
                    eng.activation(QF[:, c:c + 512], bk[:, :], ACT.Copy, scale=scl[:, 0:1])\
                        .then_inc(qk_act, 1)
                    eng.activation(PT[:, 0, c:c + 512], bk[:, :], ACT.Copy, scale=scl[:, 0:1])\
                        .then_inc(side_free[k], 1)
                    eng.wait_ge(side_free[k], at(n[f"bank{k}"] + 1))
                    eng.sem_inc(qk_act, 1)
                elif name == "H1":
                    eng.wait_ge(fe_t, at(8 * n["FE8"]))
                    bk = full(n, k)
                    eng.activation(HE[:, 0, k * 512:k * 512 + 512], bk[:, :], ACT.Relu)\
                        .then_inc(side_free[k], 1)
                    eng.wait_ge(side_free[k], at(n[f"bank{k}"] + 1))
                    eng.sem_inc(hid_ready, 1)
                    if is_last:
                        eng.sem_inc(xt_used, 1)
                elif name in ("L0", "L1"):
                    ll = int(name[1])
                    if ll == 0:
                        eng.wait_ge(wc_ready, at(b + 1))
                    bk = full(n, k)
                    for g in (2 * k, 2 * k + 1):
                        c = (g % 2) * 256
                        dst = HE[:, 1, g * 256:g * 256 + 256].rearrange("p (j q) -> p j q", j=JT) \
                            if ll == 0 else \
                            HE[:, 0, :].rearrange("p (j g q) -> p j g q", j=JT, g=G)[:, :, g, :]
                        ins = eng.activation(dst, bk[:, c:c + 256].rearrange("p (j q) -> p j q", j=JT),
                                             ACT.Relu, bias=WC[:, g, ll, HID:HID + 1])
                    ins.then_inc(side_free[k], 1)
                    eng.wait_ge(side_free[k], at(n[f"bank{k}"] + 1))
                    eng.sem_inc(hid_ready, 1)
                elif name == "MT":
                    eng.wait_ge(fe_t, at(8 * b))
                    eng.wait_ge(y_init, at(b))
                    bk = full(n, k)
                    c = k * 512
                    eng.activation(MTf[0:E, c:c + 512], bk[0:E, :], ACT.Copy).then_inc(mt_ready, 1)
                    eng.activation(MTb[0:E, c:c + 512], bk[0:E, :], ACT.Copy).then_inc(side_free[k], 1)
                    eng.wait_ge(side_free[k], at(n[f"bank{k}"] + 1))
                    eng.sem_inc(mt_ready, 1)
                elif name.startswith("FE") and k == 0 and not is_last:
                    e = int(name[2:])
                    eng.wait_ge(fe_t, at(8 * b + max(e - 1, 0)))
                    bk = full(n, 0)
                    eng.activation(mbs[:, e % 2, :], bk[:, :], ACT.Copy).then_inc(side_free[0], 1)
                    eng.wait_ge(side_free[0], at(n["bank0"] + 1))
                    eng.sem_inc(mb_ready, 1)
                elif name.startswith("FW") and is_last:
                    e = int(name[2:])
                    eng.wait_ge(fe_t, at(8 * b + max(e - 1, 0)))
                    if e == 0:
                        eng.wait_ge(h1n_ready, at(n["WO"]))
                    for k in range(2):
                        bk = full(n, k, k - 1)
                        eng.activation(HE[:, e % 2, k * 512:k * 512 + 512], bk[:, :], ACT.Gelu)\
                            .then_inc(side_free[k], 1)
                    for k in range(2):
                        eng.wait_ge(side_free[k], at(n[f"bank{k}"] + k))
                    eng.sem_inc(he_ready, 2)
                    if e == E - 1:
                        eng.sem_inc(xt_used, 1)

            def acc_out(u, si):
                acc = ACC_LAST[u]
                if acc == 0:
                    eng.wait_ge(tail_d, at(4 * si))
                g, half = acc // 2, acc % 2
                eng.wait_ge(pv_done, at(TILES * (UNITS * si + u + 1)))
                eng.activation(acc_sb[:, g, half * 512:half * 512 + 512], ACC[:, :], ACT.Copy)\
                    .then_inc(acc_free, 1)

            def body(kind, it, v0, grp, side, found):
                if kind == "serial":
                    for n, stage in enumerate(side):
                        side_stage(stage, found[(0, 0), n])
                    return
                steps, starts, ends = boundaries(kind, grp, v0, it)
                si0 = Lin(v0.k // UNITS, v0.c // UNITS) if isinstance(v0, Lin) else v0 // UNITS
                for s in range(steps):
                    for t in range(TILES):
                        m = TILES * (v0 + s) + t
                        eng.wait_ge(st_ready, at(m + 1))
                        eng.wait_ge(pv_done, at(m - TILES + 1))
                        eng.activation(prob[:, t, :], ST[t % 2][:, :], ACT.Exp).then_inc(exp_done, 1)
                        if t == 2:
                            if s > 0 and (s - 1) % UNITS in ACC_LAST:
                                acc_out((s - 1) % UNITS, si0 + (s - 1) // UNITS)
                            elif s == 0 and not starts:
                                acc_out(UNITS - 1, si0 - 1)
                        for n, stage in enumerate(side[s, t]):
                            side_stage(stage, found[(s, t), n])
                if ends:
                    acc_out(UNITS - 1, si0 + (steps - 1) // UNITS)

            run_phases(eng, reg, body)

        @block.vector
        def _(eng):
            reg = [None]
            at = counter(reg)
            done = [0]

            def step(ins):
                ins.then_inc(s_dve, 1)
                done[0] += 1
                eng.wait_ge(s_dve, done[0])

            step(eng.memset(XT[64:P, :], 0.0))
            for tile in (QA[0], KA[0]):
                ins = eng.memset(tile[64:K_ALL, :, :], 0.0)
            step(ins)
            step(eng.memset(KA[0][K_MAX:K_ALL, :, :], 1.0))
            eng.wait_ge(s_dma, N_SET_DMA[0])
            eng.wait_ge(s_pe, 2)
            for part in range(2):
                for hh in range(2):
                    src = SIDE[part][64 * hh:64 * hh + 64, :].rearrange("c (o a p) -> c a o p", a=2, p=8)
                    for a in range(2):
                        ins = eng.tensor_copy(
                            Wf[64 * hh:64 * hh + 64, :, a, 32 * part:32 * part + 32].rearrange("c j o -> c o j"),
                            src[:, a, :, 4 * hh:4 * hh + 4])
            step(ins)
            eng.tensor_copy(h0c[0:2 * WINDOW, :, :].rearrange("p j c -> p (j c)").bitcast(BF16),
                            prob[0:2 * WINDOW, 0:2, :].rearrange("p a c -> p (a c)"))
            eng.tensor_copy(ident_b[:, :], ident)
            step(eng.tensor_copy(SEL[:, :, :].rearrange("p e c -> p (e c)"),
                                 CT[:, 4 * P + 200:4 * P + 200 + 512]))
            eng.wait_ge(s_pe, 4)
            biasf = QF[0:WINDOW, :]
            for a in range(2):
                ins = eng.tensor_copy(biasf[:, a * 512:a * 512 + 512], NAT[a][0:WINDOW, :])
            step(ins)
            step(eng.tensor_copy(PT[0:WINDOW, 0, :], biasf))
            step(eng.tensor_tensor(biasf, biasf, PT[0:WINDOW, 0, :], ALU.subtract))
            step(eng.tensor_copy(PT[0:WINDOW, 1, :], biasf))
            step(eng.tensor_tensor(PT[0:WINDOW, 2, :], biasf, PT[0:WINDOW, 1, :], ALU.subtract))
            for ll in range(2):
                ins = eng.tensor_tensor(WS[:, ll, 0:HID], WS[:, ll, 0:HID], ident, ALU.add)
            step(ins)
            step(eng.memset(mpart[:, :, :, :], 0.0))
            assert done[0] == SET_DVE, done[0]
            eng.wait_ge(s_pool, SET_POOL)
            eng.wait_ge(s_dma, N_SET_DMA[1])

            def full(n, k, use=0):
                eng.wait_ge(side_full[k], at(n[f"bank{k}"] + use + 1))
                return SIDE[k]

            def nat3(bk):
                return bk[:, :].rearrange("p (j c) -> p j c", j=JT)

            def side_stage(stage, n):
                name, b, k, is_last, *more = stage
                if name == "TOKC":
                    eng.wait_ge(ho0, at(b))
                    bk = full(n, 0)
                    eng.tensor_copy(h0n[:, :, :], nat3(bk)).then_inc(side_free[0], 1)
                    eng.wait_ge(side_free[0], at(n["bank0"] + 1))
                    eng.sem_inc(h0n_ready, 1)
                elif name == "LN1":
                    src = {"0": h0n, "a": h0c, "1": h1n, "m": h1c}[more[0]]
                    k = n["LN1"]
                    eng.wait_ge(ln_p, at(6 * k))
                    if more[0] == "0":
                        eng.wait_ge(h0n_ready, at(b + 1))
                    elif more[0] == "1":
                        eng.wait_ge(h1n_ready, at(b + 1))
                    else:
                        eng.wait_ge(hres, at(n["PROJ"]))
                    eng.tensor_reduce(ln_s[:, 0, :], src[:, :, :], AX.X, ALU.add).then_inc(ln_d, 1)
                elif name == "LN2":
                    eng.wait_ge(ln_p, at(6 * n["LN2"] + 3))
                    eng.tensor_reduce(ln_s[:, 2, :], sq[:, :, :], AX.X, ALU.add).then_inc(ln_d, 1)
                elif name == "QV":
                    eng.wait_ge(vc_done, at(n["QV"]))
                    bk = full(n, 0)
                    eng.tensor_copy(Vn[:, :, :], nat3(bk)).then_inc(side_free[0], 1)
                    eng.wait_ge(side_free[0], at(n["bank0"] + 1))
                    eng.sem_inc(vn_ready, 1)
                    eng.sem_inc(xt_used, 1)
                elif name == "CR":
                    bank, c = k // 4, k % 4 * P
                    before = 4 * n["CR"] + 2 * bank
                    eng.wait_ge(side_full[bank], at(n[f"bank{bank}"]))
                    if c == 0:
                        eng.wait_ge(hres, at(n["CR"]))
                        eng.wait_ge(tail_d, at(before))
                    ins = eng.reciprocal(rec[:, c:c + P], SIDE[bank][64:P, c:c + P])
                    if k % 4 == 3:
                        ins.then_inc(tail_d, 1)
                        eng.wait_ge(tail_d, at(before + 1))
                        eng.tensor_tensor(OT[0:64, bank * 512:bank * 512 + 512], SIDE[bank][0:64, :],
                                          rec[:, :], ALU.mult).then_inc(side_free[bank], 1)
                        eng.wait_ge(side_free[bank], at(n[f"bank{bank}"]))
                        eng.sem_inc(tail_d, 1)
                elif name == "PROJ":
                    h, turn = (h0c, ho0) if more[0] == 0 else (h1c, ho1)
                    eng.wait_ge(turn, at(b + 1))
                    bk = full(n, 0)
                    eng.tensor_tensor(h[:, :, :], nat3(bk), h[:, :, :], ALU.add).then_inc(side_free[0], 1)
                    eng.wait_ge(side_free[0], at(n["bank0"] + 1))
                    eng.sem_inc(hres, 1)
                elif name == "WO":
                    eng.wait_ge(bo_done, at(b + 1))
                    eng.wait_ge(ho1, at(b))
                    bk = full(n, 0)
                    eng.tensor_tensor(h1n[:, :, :], nat3(bk), h0c[:, :, :], ALU.add).then_inc(side_free[0], 1)
                    eng.wait_ge(side_free[0], at(n["bank0"] + 1))
                    eng.sem_inc(h1n_ready, 1)
                elif name == "GATE":
                    eng.wait_ge(xt_ready, at(2 * n["TR"]))
                    bk = full(n, 0)
                    eng.tensor_copy(gs[:, :, :].rearrange("p j e -> p (j e)"), bk[:, 0:JT * E])\
                        .then_inc(side_free[0], 1)
                    eng.wait_ge(side_free[0], at(n["bank0"] + 1))
                    eng.sem_inc(gate_d, 1)
                    other = gs[:, :, :].unsqueeze(2).to_broadcast([P, JT, E, E])
                    own = gs[:, :, :].unsqueeze(3).to_broadcast([P, JT, E, E])
                    for tile, op in ((xc, ALU.is_ge), (sq, ALU.is_gt)):
                        eng.tensor_tensor(tile[:, :, :].rearrange("p j (e f) -> p j e f", e=E),
                                          other, own, op).then_inc(gate_d, 1)
                elif name == "RANK":
                    eng.wait_ge(gate_p, at(3 * (b + 1)))
                    eng.tensor_reduce(rank[:, :, :], xc[:, :, :].rearrange("p j (e f) -> p j e f", e=E),
                                      AX.X, ALU.add).then_inc(gate_d, 1)
                    eng.wait_ge(gate_d, at(5 * b + 4))
                    eng.tensor_scalar(mask[:, :, :], rank[:, :, :], 1.5, None, ALU.is_lt).then_inc(gate_d, 1)
                elif name.startswith("FE") and is_last:
                    e = int(name[2:])
                    bk = full(n, 1)
                    if e == 0:
                        eng.wait_ge(out_ready, at(b))
                        eng.tensor_copy(yacc[:, :], bk[:, :]).then_inc(side_free[1], 1)
                        eng.wait_ge(side_free[1], at(n["bank1"] + 1))
                        eng.sem_inc(y_init, 1)
                        return
                    eng.wait_ge(mb_ready, at(8 * b + e))
                    eng.wait_ge(y_add, at(8 * b + max(e - 2, 0)))
                    eng.tensor_tensor(ytmp[:, (e - 1) % 2, :], bk[:, :], mbs[:, (e - 1) % 2, :], ALU.mult)\
                        .then_inc(side_free[1], 1)
                    eng.wait_ge(side_free[1], at(n["bank1"] + 1))
                    eng.sem_inc(fe_t, 1)
                elif name == "OUT":
                    eng.wait_ge(out_dma, at(16 * b))
                    bk = full(n, 0)
                    for hf in range(2):
                        ins = eng.tensor_tensor(
                            ot[:, 4 * hf:4 * hf + 4, :],
                            bk[:, :].rearrange("p (j f d) -> p f j d", j=4, f=2)[:, hf],
                            h1c[:, 4 * hf:4 * hf + 4, :], ALU.add)
                    ins.then_inc(side_free[0], 1)
                    eng.wait_ge(side_free[0], at(n["bank0"] + 1))
                    eng.sem_inc(out_ready, 1)

            def rows_out(v0, grp, s, dma_seen, last=False):
                idx = RING_USES * v0 + (RING_USES * s + 2 * grp if not last else RING_USES * (s - 1) + 2 * grp + 1)
                place = (RING_USES * s + 2 * grp if not last else RING_USES * (s - 1) + 2 * grp + 1) % len(NAT)
                half = Lin(v0.k // 2, v0.c // 2) if isinstance(v0, Lin) else v0 // 2
                eng.wait_ge(maxrow_in[s % 2], at(16 * (half + dma_seen)))
                eng.wait_ge(nat_ready, at(idx + 1))
                eng.tensor_copy(mrow[:, s % 2, :], NAT[place][0:4 * PARTS, 0:P]).then_inc(nat_free, 1)
                eng.wait_ge(nat_free, at(idx + 1))
                eng.sem_inc(mrow_ready, 1)

            def reduce_tile(v0, grp, s, k):
                use = RING_USES * s + 2 * grp + 1 + k
                eng.wait_ge(nat_ready, at(RING_USES * v0 + use + 1))
                if k == 0:
                    eng.wait_ge(negm_ready, at(v0 + s - 1))
                eng.tensor_reduce(mx[:, s % 2, k // 2, k % 2:k % 2 + 1], NAT[use % len(NAT)][:, :], AX.X, ALU.max)\
                    .then_inc(nat_free, 1)

            def unit_max(v0, grp, s):
                eng.wait_ge(nat_free, at(RING_USES * v0 + RING_USES * s + 2 * grp + 1 + TILES))
                eng.wait_ge(parts_ready, at(v0 + s - 1))
                eng.tensor_reduce(neg_max[:, s % 2, :], mx[:, s % 2, :, :], AX.X, ALU.max, negate=True)\
                    .then_inc(negm_ready, 1)

            def body(kind, it, v0, grp, side, found):
                if kind == "serial":
                    for n, stage in enumerate(side):
                        side_stage(stage, found[(0, 0), n])
                    return
                steps, starts, ends = boundaries(kind, grp, v0, it)
                if starts:
                    for s in range(3):
                        rows_out(v0, grp, s, 0)
                        for k in range(TILES):
                            reduce_tile(v0, grp, s, k)
                        unit_max(v0, grp, s)
                for s in range(steps):
                    ahead = s + 3
                    if not (ends and s + 1 >= steps):
                        rows_out(v0, grp, ahead, ahead // 2 - 1, last=(ends and s + 2 == steps))
                    for k in range(TILES):
                        if not (ends and ahead >= steps):
                            reduce_tile(v0, grp, ahead, k)
                        for n, stage in enumerate(side[s, k]):
                            side_stage(stage, found[(s, k), n])
                    if not (ends and ahead >= steps):
                        unit_max(v0, grp, ahead)

            run_phases(eng, reg, body)

        @block.gpsimd
        def _(eng):
            reg = [None]
            at = counter(reg)

            def alone(_):
                eng.sem_inc(pool_passed, 1)

            n_set = [0]

            def clear(ap, value=0.0):
                eng.memset(ap, value).then_inc(s_pool, 1)
                n_set[0] += 1
                eng.wait_ge(s_pool, n_set[0])

            clear(QA[1][64:K_ALL, :, :])
            clear(KA[1][64:K_MAX, :, :])
            clear(KA[1][K_MAX:K_ALL, :, :], 1.0)
            for a in (0, 1):
                clear(VZ[a][:, :, :, :])
            clear(MTf[:, :])
            clear(MTb[:, :])
            clear(OT[64:P, :])
            eng.wait_ge(s_dve, 1)
            clear(XT[64:65, :], 1.0)
            clear(OT[64:65, :], 1.0)
            for a in (0, 1):
                for pos in range(3):
                    heads = [hs[pos] for hs in HEAD_GROUPS if pos < len(hs)]
                    c = ROWS_H * pos + HD
                    ins = eng.memset(VZ[a][:, :, heads[0]:heads[-1] + 1:3, c:c + 1], 1.0)
            ins.then_inc(s_pool, 1)
            eng.wait_ge(s_pool, SET_POOL)
            eng.wait_ge(s_dma, N_SET_DMA[1])

            def wide(col):
                return ln_s[:, col, :].unsqueeze(2).to_broadcast([P, JT, 64])

            def side_stage(stage, n, v0):
                name, b, _, is_last, *more = stage
                if not is_last:
                    return
                if name == "LN1":
                    src = {"0": h0n, "a": h0c, "1": h1n, "m": h1c}[more[0]]
                    k6 = 6 * n["LN1"]
                    alone(eng.wait_ge(ln_d, at(2 * n["LN1"] + 1)))
                    alone(eng.wait_ge(xt_ready, at(2 * n["LN1"])))
                    alone(eng.wait_ge(gate_d, at(5 * n["RANK"])))
                    eng.tensor_scalar(ln_s[:, 1, :], ln_s[:, 0, :], 1.0 / 64, 0.0, ALU.mult, ALU.add)\
                        .then_inc(ln_p, 1)
                    alone(eng.wait_ge(ln_p, at(k6 + 1)))
                    eng.tensor_tensor(xc[:, :, :], src[:, :, :], wide(1), ALU.subtract).then_inc(ln_p, 1)
                    alone(eng.wait_ge(ln_p, at(k6 + 2)))
                    eng.tensor_tensor(sq[:, :, :], xc[:, :, :], xc[:, :, :], ALU.mult).then_inc(ln_p, 1)
                elif name == "LN2":
                    k6 = 6 * n["LN2"]
                    alone(eng.wait_ge(ln_d, at(2 * n["LN2"] + 2)))
                    eng.tensor_scalar(ln_s[:, 3, :], ln_s[:, 2, :], 1.0 / 64, EPS, ALU.mult, ALU.add)\
                        .then_inc(ln_p, 1)
                    alone(eng.wait_ge(ln_p, at(k6 + 4)))
                    eng.tensor_tensor(ln_s[:, 4, :], ln_s[:, 3, :], half_pow, ALU.pow).then_inc(ln_p, 1)
                    alone(eng.wait_ge(ln_p, at(k6 + 5)))
                    eng.tensor_tensor(xc[:, :, :], xc[:, :, :], wide(4), ALU.mult).then_inc(ln_p, 1)
                elif name == "QK":
                    q = n["QK"]
                    alone(eng.wait_ge(qk_act, at(4 * (q + 1))))
                    eng.tensor_tensor(QF[:, :], QF[:, :], PT[:, 0, :], ALU.subtract).then_inc(split_p, 1)
                    alone(eng.wait_ge(split_p, at(3 * q + 1)))
                    eng.tensor_scalar(PT[:, 1, :], QF[:, :], 1.0, 0.0, ALU.mult, ALU.add).then_inc(split_p, 1)
                    alone(eng.wait_ge(split_p, at(3 * q + 2)))
                    eng.tensor_tensor(PT[:, 2, :], QF[:, :], PT[:, 1, :], ALU.subtract).then_inc(split_p, 1)
                elif name == "VC":
                    a, at_unit = more
                    alone(eng.wait_ge(vn_ready, at(n["VC"] + 1)))
                    alone(eng.wait_ge(pv_done, at(TILES * (v0 + at_unit))))
                    vh = Vn[:, :, :].rearrange("p j (h d) -> p j h d", d=HD)
                    for pos in range(3):
                        heads = [hs[pos] for hs in HEAD_GROUPS if pos < len(hs)]
                        sl = slice(heads[0], heads[-1] + 1, 3)
                        c = ROWS_H * pos
                        ins = eng.tensor_copy(VZ[a][:, :, sl, c:c + HD], vh[:, :, sl, :])
                    ins.then_inc(vc_done, 1)
                elif name == "HO0":
                    alone(eng.wait_ge(h1n_ready, at(b)))
                    alone(eng.wait_ge(h0n_ready, at(b + 1)))
                    eng.tensor_copy(h0c[:, :, :], h0n[:, :, :]).then_inc(ho0, 1)
                elif name == "HO1":
                    alone(eng.wait_ge(out_ready, at(b)))
                    alone(eng.wait_ge(h1n_ready, at(b + 1)))
                    eng.tensor_copy(h1c[:, :, :], h1n[:, :, :]).then_inc(ho1, 1)
                elif name == "BO":
                    eng.tensor_tensor(h0c[:, :, :], h0c[:, :, :],
                                      bob[:, :].unsqueeze(1).to_broadcast([P, JT, 64]), ALU.add)\
                        .then_inc(bo_done, 1)
                elif name == "WCA":
                    alone(eng.wait_ge(wc_in, at(16 * G * (b + 1))))
                    for g in range(G):
                        ins = eng.tensor_tensor(WC[:, g, :, :], WC[:, g, :, :], WS[:, :, :], ALU.add)
                    ins.then_inc(wc_ready, 1)
                elif name == "GATE":
                    for m, (tile, tri) in enumerate(((xc, low), (sq, upp))):
                        alone(eng.wait_ge(gate_d, at(5 * b + 2 + m)))
                        eng.tensor_tensor(tile[:, :, :], tile[:, :, :],
                                          tri.unsqueeze(1).to_broadcast([P, JT, 64]), ALU.mult)\
                            .then_inc(gate_p, 1)
                    alone(eng.wait_ge(gate_p, at(3 * b + 2)))
                    eng.tensor_tensor(xc[:, :, :], xc[:, :, :], sq[:, :, :], ALU.add).then_inc(gate_p, 1)
                elif name.startswith("FE") and name != "FE0":
                    e = int(name[2:]) - 1
                    alone(eng.wait_ge(fe_t, at(8 * b + e + 1)))
                    alone(eng.wait_ge(y_add, at(8 * b + e)))
                    alone(eng.wait_ge(y_init, at(b + 1)))
                    eng.tensor_tensor(yacc[:, :], yacc[:, :], ytmp[:, e % 2, :], ALU.add).then_inc(y_add, 1)

            def split_max(v0, grp, s):
                v = v0 + s
                alone(eng.wait_ge(negm_ready, at(v + 1)))
                alone(eng.wait_ge(nat_ready, at(RING_USES * v0 + RING_USES * s + 2 * grp + 1)))
                p, nm, rs = mpart[:, s % 2], neg_max[:, s % 2, :], mres[:, s % 2, :]
                eng.tensor_scalar(p[:, 0, :], nm, 1.0, 0.0, ALU.mult, ALU.add).then_inc(mchain, 1)
                alone(eng.wait_ge(mchain, at(3 * v + 1)))
                eng.tensor_tensor(rs, nm, p[:, 0, :], ALU.subtract).then_inc(mchain, 1)
                alone(eng.wait_ge(mchain, at(3 * v + 2)))
                eng.tensor_scalar(p[:, 1, :], rs, 1.0, 0.0, ALU.mult, ALU.add).then_inc(mchain, 1)
                alone(eng.wait_ge(mchain, at(3 * v + 3)))
                eng.tensor_tensor(p[:, 2, :], rs, p[:, 1, :], ALU.subtract).then_inc(parts_ready, 1)

            def body(kind, it, v0, grp, side, found):
                if kind == "serial":
                    for n, stage in enumerate(side):
                        side_stage(stage, found[(0, 0), n], 0)
                    return
                steps, starts, ends = boundaries(kind, grp, v0, it)
                if starts:
                    for s in range(3):
                        split_max(v0, grp, s)
                for s in range(steps):
                    for t in range(TILES):
                        for n, stage in enumerate(side[s, t]):
                            side_stage(stage, found[(s, t), n], v0)
                    if not (ends and s + 3 >= steps):
                        split_max(v0, grp, s + 3)

            run_phases(eng, reg, body)


def kernel(**inputs):
    import numpy as np
    import concourse.bacc as _bacc
    from concourse import mybir as _mybir
    from concourse.bass_utils import run_bass_kernel_spmd as _run

    inp = {k: np.asarray(v) for k, v in inputs.items()}
    f = np.float32

    def rows(*parts, n=P):
        m = np.concatenate([np.asarray(p, f).reshape(-1, p.shape[-1]) for p in parts])
        return np.concatenate([m, np.zeros((n - m.shape[0], m.shape[1]), f)])

    arrays = {}
    arrays["x"] = inp["x"]
    arrays["w_dft"] = inp["L0_tok_W"].reshape(64, 18, 64).transpose(1, 0, 2)
    ang = 2 * np.pi * np.outer(np.arange(9), np.arange(16)) / 16
    arrays["dft"] = np.concatenate([np.cos(ang), -np.sin(ang)]).astype(f) / f(4)
    tok = (np.arange(P)[None, :] * JT + np.arange(JT)[:, None]).ravel()
    hot = (tok[None, :] % WINDOW == np.arange(WINDOW)[:, None]).astype(f)
    arrays["onehot"] = np.concatenate([hot, hot])
    comb = np.zeros((3, P, P), f)
    for g, heads in enumerate(HEAD_GROUPS):
        for pos, h in enumerate(heads):
            for c in range(4):
                for d in range(HD):
                    comb[g, 32 * c + ROWS_H * pos + d, HD * h + d] = 1
                    comb[g, 32 * c + ROWS_H * pos + HD, 64 + HD * h + d] = 1
    e, o = np.arange(E)[:, None], np.arange(E)[None, :]
    low, upp = (o < e).astype(f).ravel(), (o > e).astype(f).ravel()
    sel = np.zeros((P, E, 64), f)
    for i in range(E):
        sel[i, i] = 1
    eye = np.eye(P, dtype=f)
    arrays["const"] = np.concatenate(
        [eye, *comb, np.tile(low, (P, 1)), np.tile(upp, (P, 1)), eye[:, 0:64] + eye[:, 64:128],
         np.full((P, 8), -0.5, f), sel.reshape(P, -1)], axis=1)
    arrays["qk_scale"] = np.concatenate([np.full((64, 1), HD ** -0.5, f), np.ones((64, 1), f)])
    qkv, qkvb, qkv1 = inp["L0_attn_qkv_w"].T, inp["L0_attn_qkv_b"][None, :], inp["L1_attn_qkv_w"].T
    arrays["qk_w"] = np.stack([rows(qkv[:, 0:128], qkvb[:, 0:128]), rows(qkv1[:, 0:128])])
    arrays["v_w"] = np.stack([rows(qkv[:, 128:], qkvb[:, 128:]), rows(qkv1[:, 128:])])
    arrays["pw"] = np.stack([rows(inp[f"L{a}_attn_proj_w"].T, inp[f"L{a}_attn_proj_b"][None, :])
                             for a in (0, 1)])
    arrays["wi"] = rows(inp["L0_ffn_Wi"].T, inp["L0_ffn_bi"][None, :])
    wr = np.concatenate([inp["L0_ffn_Wr"].transpose(1, 3, 0, 2),
                         inp["L0_ffn_br"].transpose(1, 2, 0)[..., None]], axis=3)
    arrays["routed"] = wr
    arrays["shared"] = np.concatenate([inp["L0_ffn_Ws"][:, 0].transpose(2, 0, 1),
                                       inp["L0_ffn_bs"][:, 0].T[..., None]], axis=2)
    arrays["wo"] = inp["L0_ffn_Wo"].T
    arrays["bo"] = inp["L0_ffn_bo"]
    arrays["table"] = inp["L0_attn_bias_table"]
    arrays["route"] = inp["L0_ffn_route_id"]
    arrays["wg"] = rows(inp["L1_ffn_Wg"], inp["L1_ffn_bg"][None, :])
    w1 = np.concatenate([inp["L1_ffn_W1"].transpose(1, 0, 2), inp["L1_ffn_b1"][None]])
    arrays["w1"] = np.concatenate([w1, np.zeros((P - 65, E, HID), f)])
    arrays["b2"] = rows(inp["L1_ffn_b2"])
    arrays["w2"] = inp["L1_ffn_W2"].transpose(1, 0, 2)
    arrays = {k: np.ascontiguousarray(v) for k, v in arrays.items()}

    nc = _bacc.Bacc("TRN2", target_bir_lowering=False, num_devices=1)
    aps = {k: nc.dram_tensor(f"in_{k}", v.shape, _mybir.dt.from_np(v.dtype), kind="ExternalInput").ap()
           for k, v in arrays.items()}
    result = nc.dram_tensor("out_h", (B, N_TOK, 64), F32, kind="ExternalOutput").ap()
    tower_kernel(nc, out=result, **aps)
    r = _run(nc, [{f"in_{k}": v for k, v in arrays.items()}], core_ids=[0])
    return r.results[0]["out_h"]
```
